# Optimizing a Trainium2 kernel written in Bass

```python
import numpy as np
import jax
import jax.numpy as jnp

def _softmax(x, axis=-1):
    return jax.nn.softmax(x, axis=axis)

def _gelu(x):
    return jax.nn.gelu(x, approximate=True)

def _silu(x):
    return jax.nn.silu(x)

def _sigmoid(x):
    return jax.nn.sigmoid(x)

def _layernorm(x, axis=-1, eps=1e-05):
    m = jnp.mean(x, axis=axis, keepdims=True)
    v = jnp.var(x, axis=axis, keepdims=True)
    return (x - m) / jnp.sqrt(v + eps)

def _scatter_add(tgt, idx, src, axis=0):
    return tgt.at[idx].add(src)

def _segment_sum(src, seg, n):
    return jax.ops.segment_sum(src, seg, n)
kernel_name = 'mk_seq_preln_d1_jaxref_r8_4eab13'

def setup_inputs(seed: int=0):
    np.random.seed(seed)
    _w = jnp.asarray

    def _L0_attn_setup():
        import jax, jax.numpy as jnp
        import numpy as np
        EMBED_DIM = 128
        BLOCK_SIZE = 256
        key = jax.random.key(seed)
        kx, kk, kq, kv = jax.random.split(key, 4)
        s = 1.0 / np.sqrt(EMBED_DIM)
        x = jax.random.normal(kx, (4, BLOCK_SIZE, EMBED_DIM), dtype=jnp.float32)
        Wk = jax.random.uniform(kk, (EMBED_DIM, EMBED_DIM), jnp.float32, -s, s)
        Wq = jax.random.uniform(kq, (EMBED_DIM, EMBED_DIM), jnp.float32, -s, s)
        Wv = jax.random.uniform(kv, (EMBED_DIM, EMBED_DIM), jnp.float32, -s, s)
        return {'x': x, 'Wk': Wk, 'Wq': Wq, 'Wv': Wv}
    _L0_attn_in = _L0_attn_setup()

    def _L0_ffn_setup():
        import jax, jax.numpy as jnp
        import numpy as np
        B, S, DIM = (2, 256, 128)
        HID = 256
        E, NSH, TOPK = (8, 2, 2)

        def _ffn(x, w1, w2, w3):
            return jax.nn.silu(x @ w1.T) * (x @ w3.T) @ w2.T
        key = jax.random.key(seed)
        ks = jax.random.split(key, 8)
        sc = 0.02
        return {'x': jax.random.normal(ks[0], (B, S, DIM), jnp.float32), 'router_w': jax.random.normal(ks[1], (E, DIM), jnp.float32) * sc, 'expert_bias': jnp.zeros((E,), jnp.float32), 'w1': jax.random.normal(ks[2], (E, HID, DIM), jnp.float32) * sc, 'w3': jax.random.normal(ks[3], (E, HID, DIM), jnp.float32) * sc, 'w2': jax.random.normal(ks[4], (E, DIM, HID), jnp.float32) * sc, 'sw1': jax.random.normal(ks[5], (NSH, HID, DIM), jnp.float32) * sc, 'sw3': jax.random.normal(ks[6], (NSH, HID, DIM), jnp.float32) * sc, 'sw2': jax.random.normal(ks[7], (NSH, DIM, HID), jnp.float32) * sc}
    _L0_ffn_in = _L0_ffn_setup()
    _d = {'L0_attn_x': _L0_attn_in['x'], 'L0_attn_Wk': _L0_attn_in['Wk'], 'L0_attn_Wq': _L0_attn_in['Wq'], 'L0_attn_Wv': _L0_attn_in['Wv'], 'L0_ffn_router_w': _L0_ffn_in['router_w'], 'L0_ffn_expert_bias': _L0_ffn_in['expert_bias'], 'L0_ffn_w1': _L0_ffn_in['w1'], 'L0_ffn_w3': _L0_ffn_in['w3'], 'L0_ffn_w2': _L0_ffn_in['w2'], 'L0_ffn_sw1': _L0_ffn_in['sw1'], 'L0_ffn_sw3': _L0_ffn_in['sw3'], 'L0_ffn_sw2': _L0_ffn_in['sw2']}
    _x0 = _d['L0_attn_x']
    _d['L0_attn_x'] = jax.random.normal(jax.random.fold_in(jax.random.key(seed), 1), (4, 1024, 128), dtype=_x0.dtype)
    del _x0
    return _d

def reference(L0_attn_x, L0_attn_Wk, L0_attn_Wq, L0_attn_Wv, L0_ffn_router_w, L0_ffn_expert_bias, L0_ffn_w1, L0_ffn_w3, L0_ffn_w2, L0_ffn_sw1, L0_ffn_sw3, L0_ffn_sw2):

    def _L0_attn_ref(x, Wk, Wq, Wv):
        import jax, jax.numpy as jnp
        import numpy as np
        EMBED_DIM = 128
        BLOCK_SIZE = 256
        B, T, C = x.shape
        K = jnp.einsum('btc,kc->btk', x, Wk)
        Q = jnp.einsum('btc,kc->btk', x, Wq)
        V = jnp.einsum('btc,kc->btk', x, Wv)
        scores = jnp.einsum('bqc,bkc->bqk', Q, K) / jnp.sqrt(jnp.float32(C))
        causal = jnp.tril(jnp.ones((T, T), dtype=bool))
        scores = jnp.where(causal, scores, -jnp.inf)
        weights = jax.nn.softmax(scores, axis=-1)
        out = jnp.einsum('bqk,bkc->bqc', weights, V)
        return out

    def _L0_ffn_ref(x, router_w, expert_bias, w1, w3, w2, sw1, sw3, sw2):
        import jax, jax.numpy as jnp
        import numpy as np
        B, S, DIM = (2, 256, 128)
        HID = 256
        E, NSH, TOPK = (8, 2, 2)

        def _ffn(x, w1, w2, w3):
            return jax.nn.silu(x @ w1.T) * (x @ w3.T) @ w2.T
        bs, sl, d = x.shape
        xf = x.reshape(-1, d)
        shared = jnp.zeros_like(xf)
        for i in range(sw1.shape[0]):
            shared = shared + _ffn(xf, sw1[i], sw2[i], sw3[i])
        logits = xf @ router_w.T + expert_bias
        rw, sel = jax.lax.top_k(logits, TOPK)
        rw = jax.nn.softmax(rw.astype(jnp.float32), axis=-1).astype(x.dtype)
        onehot = jax.nn.one_hot(sel, E, dtype=x.dtype)
        combine = jnp.einsum('tk,tke->te', rw, onehot)

        def body(acc, ew):
            e1, e3, e2, cw = ew
            acc = acc + cw[:, None] * _ffn(xf, e1, e2, e3)
            return (acc, None)
        out, _ = jax.lax.scan(body, jnp.zeros_like(xf), (w1, w3, w2, combine.T))
        out = out + shared
        return out.reshape(bs, sl, -1)
    x = L0_attn_x
    x = x + _L0_attn_ref(_layernorm(x, axis=-1), L0_attn_Wk, L0_attn_Wq, L0_attn_Wv)
    x = x + _L0_ffn_ref(_layernorm(x, axis=-1), L0_ffn_router_w, L0_ffn_expert_bias, L0_ffn_w1, L0_ffn_w3, L0_ffn_w2, L0_ffn_sw1, L0_ffn_sw3, L0_ffn_sw2)
    return x

_drawn_inputs = setup_inputs


def setup_inputs(seed=0):
    import zlib

    import numpy as np

    out = dict(_drawn_inputs(seed))
    spreads = {'L0_ffn_expert_bias': (0.0, 0.8)}
    factors = {'L0_ffn_router_w': 8.0,
     'L0_ffn_w1': 8.0,
     'L0_ffn_w3': 8.0,
     'L0_ffn_w2': 8.0,
     'L0_ffn_sw1': 4.847,
     'L0_ffn_sw3': 4.826,
     'L0_ffn_sw2': 4.836}
    for name, (base, spread) in spreads.items():
        noise = np.random.default_rng([zlib.crc32(name.encode()), seed]).standard_normal(out[name].shape)
        drawn = base * np.exp(spread * noise) if base else spread * noise
        out[name] = jnp.asarray(drawn.astype(out[name].dtype))
    for name, factor in factors.items():
        out[name] = (out[name] * factor).astype(out[name].dtype)
    return out
```

```python
from contextlib import ExitStack

import concourse.bass as bass
from concourse import mybir

F32 = mybir.dt.float32
F32R = mybir.dt.float32r
BF16 = mybir.dt.bfloat16
I32 = mybir.dt.int32
U32 = mybir.dt.uint32
ALU = mybir.AluOpType
ACT = mybir.ActivationFunctionType
AXX = mybir.AxisListType.X

P = 128
CREDIT = 2
EPS = 1e-5
MASKED = -3.0e38


def done(n):
    return n + 1 + CREDIT


class Chain:

    def __init__(self, eng, sem, per):
        self.eng, self.sem, self.per = eng, sem, per

    def start(self, n):
        self.base, self.k = CREDIT + n * self.per, 0

    def inc(self, ins):
        self.k += 1
        ins.then_inc(self.sem, 1)

    def link(self, ins):
        self.inc(ins)
        self.wait()

    def wait(self):
        self.eng.wait_ge(self.sem, self.base + self.k)

    def end(self):
        self.wait()
        assert self.k == self.per, self.k


def build(nc, x, wk, wq, wv, router_w, expert_bias, w1, w3, w2, sw1, sw3, sw2, out, xbuf, ybuf):
    B, T, C = x.shape
    E, HID, _ = w1.shape
    NSH = sw1.shape[0]
    NX = NSH + E
    NTOK = B * T
    NT = NTOK // P
    TB = T // P
    KTOP = 2
    REGION = NTOK + P
    ROW = C + 2
    SLOTS = 4 * -(-((KTOP * NTOK + E * (P - 1)) // P) // 4)
    PAIRS = SLOTS // 2
    SPARE = SLOTS - KTOP * NTOK // P
    GT = 4
    NG = NT // GT
    WCOLS = 2 * HID + HID // P * C
    WBLK = WCOLS // P
    SCALE = float(C) ** -0.5
    assert C == P and HID == 2 * P and SPARE <= 8

    x_rows = x.rearrange("b (t p) c -> p (b t) c", p=P)
    out_rows = out.rearrange("b (t p) c -> p (b t) c", p=P)

    with ExitStack() as ctx:
        def sb(name, shape, dt=F32):
            return ctx.enter_context(nc.sbuf_tensor(name, shape, dt))

        def sem(name):
            return ctx.enter_context(nc.semaphore(name))

        x_all = sb("x_all", [P, NT, C])
        w_hi = sb("w_hi", [P, NX, WCOLS], F32R)
        w_lo = sb("w_lo", [P, NX, WCOLS], F32R)
        raw = [sb(f"raw{n}", [P, WBLK, P]) for n in range(2)]
        wqkv = sb("wqkv", [P, 3, C])
        rw_raw = sb("rw_raw", [P, C])
        bias_col = sb("bias_col", [E, 1])
        SM = 3 * C
        sm_hi = sb("sm_hi", [P, SM], F32R)
        sm_lo = sb("sm_lo", [P, SM], F32R)
        ident = sb("ident", [P, P])
        ident_b = sb("ident_b", [P, P], BF16)
        ones_b = sb("ones_b", [P, P], BF16)
        upper_b = sb("upper_b", [P, P], BF16)
        mask_b = sb("mask_b", [P, P], BF16)
        mhalf = sb("mhalf", [P, TB])
        iota_e = sb("iota_e", [P, E])
        region0 = sb("region0", [P, E])
        padrow = sb("padrow", [P, ROW])
        part_id = sb("part_id", [P, 1])
        row_id = sb("row_id", [P, KTOP, NT], I32)

        stats = sb("stats", [P, TB, 6])
        mv = sb("mv", [P, NT, 2])
        rstd = sb("rstd", [P, NT])
        veps = sb("veps", [P, NT])
        xn = sb("xn", [P, TB, C])
        xT_hi = sb("xT_hi", [P, T], F32R)
        xT_lo = sb("xT_lo", [P, T], F32R)
        yT_hi = sb("yT_hi", [P, T], F32R)
        yT_lo = sb("yT_lo", [P, T], F32R)
        v_hi = sb("v_hi", [P, T], F32R)
        v_lo = sb("v_lo", [P, T], F32R)
        prob = [sb(f"prob{n}", [P, T]) for n in range(2)]
        pT_hi = [sb(f"pT_hi{n}", [P, T], F32R) for n in range(2)]
        pT_lo = [sb(f"pT_lo{n}", [P, T], F32R) for n in range(2)]
        nmax = sb("nmax", [P, TB])
        rsum = sb("rsum", [P, TB])
        rinv = sb("rinv", [P, TB])

        mv2 = sb("mv2", [P, GT, 2])
        rstd2 = sb("rstd2", [P, GT])
        veps2 = sb("veps2", [P, GT])
        xrow = [[sb(f"xrow{k}{n}", [P, GT, ROW]) for n in range(2)] for k in range(KTOP)]
        x2T_hi = [sb(f"x2T_hi{n}", [P, GT * P], F32R) for n in range(2)]
        x2T_lo = [sb(f"x2T_lo{n}", [P, GT * P], F32R) for n in range(2)]
        logitT = sb("logitT", [E, GT * P])
        logit = sb("logit", [P, GT, E])
        top = sb("top", [P, GT, 8])
        topi = sb("topi", [P, GT, 8], U32)
        topf = sb("topf", [P, GT, KTOP])
        hot = [sb(f"hot{k}", [P, GT, E]) for k in range(KTOP)]
        hot_b = sb("hot_b", [P, GT, E], BF16)
        gap = sb("gap", [P, GT])
        gapt = sb("gapt", [P, GT])
        count = sb("count", [P, E])
        added = sb("added", [P, E])
        place = sb("place", [P, GT, E])
        picked = sb("picked", [P, GT, E])
        posf = sb("posf", [P, GT])
        pos = [[sb(f"pos{k}{n}", [P, GT], I32) for n in range(2)] for k in range(KTOP)]
        sil = [sb(f"sil{n}", [P, 512]) for n in range(2)]
        hid = [sb(f"hid{n}", [P, 512]) for n in range(2)]
        hT_hi = [sb(f"hT_hi{n}", [P, 512], F32R) for n in range(2)]
        hT_lo = [sb(f"hT_lo{n}", [P, 512], F32R) for n in range(2)]
        shT = sb("shT", [P, GT * P])

        padpos = sb("padpos", [P, E], I32)
        padposf = sb("padposf", [P, E])
        t8 = [sb(f"t8_{n}", [1, E]) for n in range(5)]
        t8i = sb("t8i", [1, E], I32)
        lower = sb("lower", [1, E, E])
        t64 = sb("t64", [1, E, E])
        iota_s = sb("iota_s", [1, SLOTS])
        past = sb("past", [1, SLOTS, E])
        past2 = sb("past2", [1, SLOTS, E])
        slot_e = sb("slot_e", [1, SLOTS])
        slot_t = sb("slot_t", [1, SLOTS])
        slot_w = sb("slot_w", [1, SLOTS])
        slot_r = sb("slot_r", [1, SLOTS])
        slot_wi = sb("slot_wi", [1, SLOTS], I32)
        slot_ri = sb("slot_ri", [1, SLOTS], I32)
        xg = sb("xg", [P, 4, ROW])
        meta = sb("meta", [P, SLOTS, 2])
        gT_hi = [sb(f"gT_hi{n}", [P, 2 * P], F32R) for n in range(2)]
        gT_lo = [sb(f"gT_lo{n}", [P, 2 * P], F32R) for n in range(2)]
        yrow = [sb(f"yrow{n}", [P, C]) for n in range(4)]
        yid = [sb(f"yid{n}", [P, 1], I32) for n in range(4)]
        NC = 4
        CT = NT // NC
        assert CT == TB
        yb = [[prob[n][:].rearrange("p (t c) -> p t c", c=C) for n in range(2)], [xn[:], sb("yb11", [P, CT, C])[:]]]

        ps = ctx.enter_context(nc.psum_tensor("ps", [P, 8 * 512], F32))

        def bank(n, cols=512, first=0):
            return ps[:, n * 512 + first:n * 512 + first + cols]

        def tile_of(a, t):
            return a[:, bass.ds(t, 1), :].rearrange("p o c -> p (o c)")

        def halves(a, k):
            return a.rearrange("p (s h) -> p s h", s=2)[:, :, k * HID:(k + 1) * HID]

        def alone(eng):
            eng.sem_inc(S["passed"], 1)

        s_x = [sem(f"s_xin{b}") for b in range(B)]
        s_small = sem("s_small")
        s_raw = [sem(f"s_raw{n}") for n in range(2)]
        s_pad0 = sem("s_pad0")
        s_rows = [sem(f"s_rows{n}") for n in range(2)]
        s_padw = sem("s_padw")
        s_xg = [sem(f"s_xg{n}") for n in range(4)]
        s_yw = [sem(f"s_yw{n}") for n in range(4)]
        s_yb = [sem(f"s_yb{n}") for n in range(NC)]
        s_out = sem("s_out")
        names = ("c_const c_norm2 c_yid c_st1 c_rinv c_st2 c_rt1 c_rt2 c_tab c_cnt c_n2 zeroed pow1 pow2 passed const wT whi wlo smT smhi smlo st1 norm1 score nmax prob pT pThi pTlo pv x2 "
                 "fill fhi flo st2 norm2 t2 t2hi t2lo lt lthi r3 rt1 rk rt2 tanh rows_sent "
                 "gu silu mul hhi hlo yT yThi back addb tab routed tx xhi xlo emeta eh esilu emul eth ehhi ehlo ey eyout "
                 "ysent yall fin0 fin").split()
        S = {n: sem("s_" + n) for n in names}

        block = ctx.enter_context(nc.Block())

        def credit(eng, *which):
            for n in which:
                eng.sem_inc(S[n], CREDIT)

        @block.sync
        def _(sp):
            for b in range(B):
                sp.dma_start(x_all[:, b * TB:(b + 1) * TB, :], x_rows[:, b * TB:(b + 1) * TB, :]).then_inc(s_x[b], 16)
                if b == 0:
                    for n, w in enumerate((wq, wk, wv)):
                        sp.dma_start(wqkv[:, n, :], w).then_inc(s_small, 16)
                    sp.wait_ge(S["zeroed"], 1)
                    sp.dma_start(rw_raw[0:E, :], router_w).then_inc(s_small, 16)
                    sp.dma_start(bias_col[:], expert_bias.rearrange("(e o) -> e o", o=1)).then_inc(s_small, 16)

            def load_expert(n, par, a1, a3, a2):
                sp.wait_ge(S["wT"], done(n - 2))
                sp.dma_start(raw[par][:, 0:2, :], a1.rearrange("o (j p) c -> p (o j) c", p=P)).then_inc(s_raw[par], 16)
                sp.dma_start(raw[par][:, 2:4, :], a3.rearrange("o (j p) c -> p (o j) c", p=P)).then_inc(s_raw[par], 16)
                sp.dma_start(raw[par][:, 4:6, :].rearrange("p j c -> p (j c)"),
                             a2.rearrange("o p h -> p (o h)")).then_inc(s_raw[par], 16)

            for n in range(NSH):
                load_expert(n, n % 2, sw1[n:n + 1], sw3[n:n + 1], sw2[n:n + 1])
            with sp.Fori(0, E // 2) as i:
                for k in range(2):
                    e = bass.ds(2 * i + k, 1)
                    load_expert(NSH + 2 * i + k, k, w1[e, :, :], w3[e, :, :], w2[e, :, :])
            sp.wait_ge(S["const"], 1)
            for n in range(8):
                r = E * REGION + n * P
                sp.dma_start(xbuf[r:r + P, :], padrow[:]).then_inc(s_pad0, 16)

            sp.wait_ge(s_pad0, 8 * 16)
            sp.wait_ge(S["tab"], 1)
            sp.wait_ge(S["routed"], 1)

            def load_slots(i, off):
                p, par = 2 * i + off, off % 2
                sp.wait_ge(S["tx"], done(p - 2))
                sp.wait_ge(S["emeta"], done(p - 2))
                for k in range(2):
                    r = sp.value_load(slot_ri[0:1, bass.ds(2 * p + k, 1)], min_val=0, max_val=E * REGION + 7 * P)
                    q = 2 * par + k
                    sp.dma_start(xg[:, q, :], xbuf[bass.ds(r, P), :]).then_inc(s_xg[q], 16)

            with sp.Fori(0, PAIRS // 2) as i:
                load_slots(i, 0)
                load_slots(i, 1)

            sp.wait_ge(S["yall"], 1)
            for n in range(NC):
                if n >= 2:
                    sp.wait_ge(S["fin"], done(n - 2))
                for k in range(KTOP):
                    src = ybuf[k * NTOK + n * CT * P:k * NTOK + (n + 1) * CT * P, :]
                    sp.dma_start(yb[k][n % 2], src.rearrange("(t p) c -> p t c", p=P)).then_inc(s_yb[n], 16)
                if n >= 1:
                    sp.wait_ge(S["fin"], done(n - 1))
                    sp.dma_start(out_rows[:, (n - 1) * CT:n * CT, :], x_all[:, (n - 1) * CT:n * CT, :]).then_inc(s_out, 16)
            sp.wait_ge(S["fin"], done(NC - 1))
            sp.dma_start(out_rows[:, (NC - 1) * CT:NT, :], x_all[:, (NC - 1) * CT:NT, :]).then_inc(s_out, 16)
            sp.wait_ge(s_out, NC * 16)

        @block.gpsimd
        def _(pl):
            credit(pl, "c_const", "c_norm2", "c_yid", "pow1", "pow2", "ysent", "fin0")

            pl.memset(rw_raw[:], 0.0).then_inc(S["zeroed"], 1)
            cc = Chain(pl, S["c_const"], 0)
            cc.start(0)
            for a, value in ((ident, 0.0), (ident_b, 0.0), (ones_b, 1.0), (upper_b, 0.0), (mask_b, 0.0), (mhalf, -0.5),
                             (lower, 1.0), (padrow, 0.0)):
                cc.inc(pl.memset(a[:], value))
            for a, pattern, per_part in ((iota_e, [[1, E]], 0), (region0, [[REGION, E]], 0), (part_id, [[0, 1]], 1),
                                         (iota_s, [[1, SLOTS]], 0), (row_id, [[NTOK, KTOP], [P, NT]], 1)):
                cc.inc(pl.iota(a[:], pattern=pattern, base=0, channel_multiplier=per_part,
                               allow_small_or_imprecise_dtypes=True))
            cc.wait()
            for a in (ident, ident_b):
                cc.inc(pl.affine_select(out=a[:], in_=a[:], compare_op=ALU.not_equal, fill=1.0, base=0,
                                        pattern=[[-1, P]], channel_multiplier=1))
            for a, fill in ((upper_b, 1.0), (mask_b, MASKED)):
                cc.inc(pl.affine_select(out=a[:], in_=a[:], compare_op=ALU.is_ge, fill=fill, base=0,
                                        pattern=[[-1, P]], channel_multiplier=1))
            cc.inc(pl.affine_select(out=lower[:], in_=lower[:], compare_op=ALU.is_ge, fill=0.0, base=0,
                                    pattern=[[1, E], [-1, E]], channel_multiplier=0))
            cc.inc(pl.iota(padrow[:, C:C + 1].bitcast(I32), pattern=[[0, 1]], base=KTOP * NTOK, channel_multiplier=0))
            cc.wait()
            pl.nop().then_inc(S["const"], 1)

            for b in range(B):
                bt = slice(b * TB, (b + 1) * TB)
                pl.wait_ge(S["st1"], done(b))
                pl.tensor_tensor(rstd[:, bt], veps[:, bt], mhalf[:], ALU.pow).then_inc(S["pow1"], 1)

            c2 = Chain(pl, S["c_norm2"], 3)

            def norm2(i, off):
                g, par = 2 * i + off, off % 2
                c2.start(g)
                pl.wait_ge(S["st2"], done(g))
                pl.tensor_tensor(rstd2[:], veps2[:], mhalf[:, 0:GT], ALU.pow).then_inc(S["pow2"], 1)
                pl.wait_ge(S["norm2"], done(g))
                alone(pl)
                c2.inc(pl.tensor_copy(xrow[1][par][:, :, 0:C], xrow[0][par][:, :, 0:C]))
                for k in range(KTOP):
                    c2.inc(pl.tensor_copy(xrow[k][par][:, :, C].bitcast(I32), row_id[:, k, bass.ds(g * GT, GT)]))
                c2.end()

            def send(i, off):
                g, par = 2 * i + off, off % 2
                pl.wait_ge(S["rt2"], done(g))
                alone(pl)
                for t in range(GT):
                    for k in range(KTOP):
                        pl.indirect_dma_start(
                            out=xbuf, out_offset=bass.IndirectOffsetOnAxis(ap=pos[k][par][:, t:t + 1], axis=0),
                            in_=xrow[k][par][:, t, :], in_offset=None).then_inc(s_rows[par], 16)

            def sent(i, off):
                pl.wait_ge(s_rows[off % 2], (i + off // 2 + 1) * GT * KTOP * 16)

            norm2(0, 0)
            norm2(0, 1)
            send(0, 0)
            sent(0, 0)
            with pl.Fori(0, NG // 2 - 1) as i:
                norm2(i, 2)
                send(i, 1)
                sent(i, 1)
                norm2(i, 3)
                send(i, 2)
                sent(i, 2)
            send(NG // 2 - 1, 1)
            pl.wait_ge(S["tab"], 1)
            for e in range(E):
                pl.indirect_dma_start(out=xbuf, out_offset=bass.IndirectOffsetOnAxis(ap=padpos[:, e:e + 1], axis=0),
                                      in_=padrow[:], in_offset=None).then_inc(s_padw, 16)
            sent(NG // 2 - 1, 1)
            pl.wait_ge(s_padw, E * 16)
            pl.nop().then_inc(S["routed"], 1)


            c3 = Chain(pl, S["c_yid"], 2)

            def send_y(i, off):
                p, par = 2 * i + off, off % 2
                c3.start(p)
                pl.wait_ge(S["emeta"], done(p))
                for k in range(2):
                    c3.inc(pl.tensor_copy(yid[2 * par + k][:], meta[:, bass.ds(2 * p + k, 1), 0].bitcast(I32)))
                c3.end()
                for k in range(2):
                    q = 2 * par + k
                    pl.wait_ge(S["eyout"], done(2 * p + k))
                    alone(pl)
                    pl.indirect_dma_start(out=ybuf, out_offset=bass.IndirectOffsetOnAxis(ap=yid[q][:], axis=0),
                                          in_=yrow[q][:], in_offset=None, bounds_check=KTOP * NTOK - 1,
                                          oob_is_err=False).then_inc(s_yw[q], 16)

            def sent_y(i, off):
                for k in range(2):
                    pl.wait_ge(s_yw[2 * (off % 2) + k], (i + off // 2 + 1) * 16)
                pl.nop().then_inc(S["ysent"], 1)

            send_y(0, 0)
            with pl.Fori(0, PAIRS // 2 - 1) as i:
                send_y(i, 1)
                sent_y(i, 0)
                send_y(i, 2)
                sent_y(i, 1)
            send_y(PAIRS // 2 - 1, 1)
            sent_y(PAIRS // 2 - 1, 0)
            sent_y(PAIRS // 2 - 1, 1)
            pl.nop().then_inc(S["yall"], 1)

            for n in range(NC):
                pl.wait_ge(s_yb[n], 2 * 16)
                pl.tensor_tensor(yb[0][n % 2], yb[0][n % 2], yb[1][n % 2], ALU.add).then_inc(S["fin0"], 1)

        @block.scalar
        def _(act):
            credit(act, "whi", "smhi", "prob", "pThi", "fhi", "t2hi", "lthi", "tanh", "silu", "hhi", "yThi",
                   "xhi", "esilu", "ehhi")

            def w_split(n, par):
                act.wait_ge(S["wT"], done(n))
                act.activation(tile_of(w_hi, n), bank(2 * par, WCOLS), ACT.Copy).then_inc(S["whi"], 1)

            act.wait_ge(S["smT"], done(0))
            for n, factor in enumerate((1.0, SCALE, 1.0)):
                act.activation(sm_hi[:, n * C:(n + 1) * C], bank(7, C, n * C), ACT.Copy, scale=factor).then_inc(S["smhi"], 1)
            for n in range(NSH):
                w_split(n, n % 2)
            with act.Fori(0, E // 2) as i:
                for k in range(2):
                    w_split(NSH + 2 * i + k, k)

            def fill_hi(b, f):
                act.wait_ge(S["fill"], done(6 * b + f))
                dst = (xT_hi, yT_hi, v_hi)[f // 2]
                if f < 4:
                    act.wait_ge(S["score"], done(TB * b - 1))
                else:
                    act.wait_ge(S["pv"], done(TB * b - 1))
                act.activation(dst[:, f % 2 * 512:f % 2 * 512 + 512], bank((7, 1)[f % 2]), ACT.Copy).then_inc(S["fhi"], 1)

            def exp(b, i):
                n = TB * b + i
                act.wait_ge(S["nmax"], done(n))
                act.wait_ge(S["pT"], done(n - 2))
                act.wait_ge(S["x2"], done(TB * b - 1))
                act.activation(prob[i % 2][:, 0:(i + 1) * P], bank(2 * (i % 2), (i + 1) * P), ACT.Exp,
                               bias=nmax[:, i:i + 1], accum_out=rsum[:, i:i + 1]).then_inc(S["prob"], 1)

            def pT_split(b, i):
                n = TB * b + i
                act.wait_ge(S["pT"], done(n))
                act.wait_ge(S["pv"], done(n - 2))
                act.activation(pT_hi[i % 2][:, 0:(i + 1) * P], bank(4, (i + 1) * P), ACT.Copy).then_inc(S["pThi"], 1)

            def batch_act(b, more):
                for i in range(TB):
                    exp(b, i)
                    if i >= 1:
                        pT_split(b, i - 1)
                if more:
                    fill_hi(b + 1, 0)
                    fill_hi(b + 1, 1)
                pT_split(b, TB - 1)
                if more:
                    for f in range(2, 6):
                        fill_hi(b + 1, f)

            for f in range(6):
                fill_hi(0, f)
            with act.Fori(0, B - 1) as b:
                batch_act(b, True)
            batch_act(B - 1, False)

            def t2_hi(i, off):
                g = 2 * i + off
                act.wait_ge(S["t2"], done(g))
                act.activation(x2T_hi[off % 2][:], bank(6), ACT.Copy).then_inc(S["t2hi"], 1)

            def lt_bias(i, off):
                g = 2 * i + off
                act.wait_ge(S["lt"], done(g))
                act.wait_ge(S["r3"], done(g - 1))
                act.activation(logitT[:], bank(6)[0:E, :], ACT.Identity, bias=bias_col[:]).then_inc(S["lthi"], 1)

            def unit_silu(g, u):
                n = 4 * g + u
                act.wait_ge(S["gu"], done(n))
                act.wait_ge(S["mul"], done(n - 2))
                act.activation(sil[u % 2][:], bank(2 * (u % 2)), ACT.Silu).then_inc(S["silu"], 1)

            def unit_hi(g, u):
                n = 4 * g + u
                act.wait_ge(S["mul"], done(n))
                act.wait_ge(S["yT"], done(n - 2))
                act.activation(hT_hi[u % 2][:], hid[u % 2][:], ACT.Copy).then_inc(S["hhi"], 1)

            def shared_act(i, off, more):
                g = 2 * i + off
                unit_silu(g, 0)
                unit_silu(g, 1)
                unit_hi(g, 0)
                act.wait_ge(S["rt1"], done(g))
                act.activation(gapt[:], gap[:], ACT.Tanh, scale=0.5).then_inc(S["tanh"], 1)
                unit_silu(g, 2)
                unit_hi(g, 1)
                if more:
                    t2_hi(i, off + 1)
                unit_silu(g, 3)
                unit_hi(g, 2)
                if more:
                    lt_bias(i, off + 1)
                unit_hi(g, 3)
                act.wait_ge(S["yT"], done(4 * g + 3))
                act.wait_ge(S["back"], done(g - 1))
                act.activation(shT[:], bank(4), ACT.Copy).then_inc(S["yThi"], 1)

            t2_hi(0, 0)
            lt_bias(0, 0)
            with act.Fori(0, NG // 2 - 1) as i:
                shared_act(i, 0, True)
                shared_act(i, 1, True)
            shared_act(NG // 2 - 1, 0, True)
            shared_act(NG // 2 - 1, 1, False)

            def x_hi(i, off):
                p, par = 2 * i + off, off % 2
                act.wait_ge(S["tx"], done(p))
                act.wait_ge(S["eh"], done(p - 2))
                act.activation(gT_hi[par][:], bank(4, 2 * P), ACT.Copy).then_inc(S["xhi"], 1)

            def e_silu(i, off):
                p, par = 2 * i + off, off % 2
                act.wait_ge(S["eh"], done(p))
                act.wait_ge(S["emul"], done(p - 2))
                act.activation(sil[par][:].rearrange("p (s h) -> p s h", s=2),
                               halves(ps[:, 1024 * par:1024 * par + 1024], 0),
                               ACT.Silu).then_inc(S["esilu"], 1)

            def h_hi(i, off):
                p, par = 2 * i + off, off % 2
                act.wait_ge(S["eth"], done(p))
                act.wait_ge(S["ey"], done(p - 2))
                act.activation(hT_hi[par][:], bank(5), ACT.Copy).then_inc(S["ehhi"], 1)

            def e_step(i, off, x=True, h=True):
                if x:
                    x_hi(i, off + 2)
                if h:
                    e_silu(i, off + 1)
                h_hi(i, off)

            x_hi(0, 0)
            x_hi(0, 1)
            e_silu(0, 0)
            e_step(0, 0)
            with act.Fori(0, PAIRS // 2 - 2) as i:
                e_step(i, 1)
                e_step(i, 2)
            L = PAIRS // 2 - 1
            e_step(L - 1, 1)
            e_step(L, 0, x=False)
            e_step(L, 1, x=False, h=False)

        @block.vector
        def _(ve):
            credit(ve, "norm1", "norm2", "c_st1", "c_rinv", "c_st2", "c_rt1", "c_rt2", "c_tab", "c_cnt", "c_n2", "wlo", "smlo", "st1", "nmax", "pTlo", "x2", "flo", "st2", "t2lo", "rt1", "rt2",
                   "mul", "hlo", "addb", "xlo", "emeta", "emul", "ehlo", "eyout", "fin")

            c1 = Chain(ve, S["c_st1"], 2 * TB)
            for b in range(B):
                c1.start(b)
                ve.wait_ge(s_x[b], 16)
                with ve.Fori(0, TB) as t:
                    ve.bn_stats(tile_of(stats, t), tile_of(x_all, b * TB + t)).then_inc(S["c_st1"], 1)
                c1.k = TB
                c1.wait()
                for t in range(TB):
                    c1.inc(ve.bn_aggr(mv[:, b * TB + t, :], stats[:, t, :]))
                c1.end()
                bt = slice(b * TB, (b + 1) * TB)
                ve.tensor_scalar(veps[:, bt], mv[:, bt, 1], EPS, None, ALU.add).then_inc(S["st1"], 1)

            def normalise(b):
                ve.wait_ge(S["pow1"], done(b))
                ve.wait_ge(S["fill"], done(6 * b - 2))
                for t in range(TB):
                    n = bass.ds(b * TB + t, 1)
                    ve.tensor_scalar(xn[:, t, :], tile_of(x_all, b * TB + t), mv[:, n, 0], rstd[:, n],
                                     ALU.subtract, ALU.mult).then_inc(S["norm1"], 1)

            ve.wait_ge(S["smhi"], done(2))
            for n, factor in enumerate((1.0, SCALE, 1.0)):
                c = slice(n * C, (n + 1) * C)
                ve.scalar_tensor_tensor(out=sm_lo[:, c], in0=bank(7, C, n * C), scalar=factor, in1=sm_hi[:, c].bitcast(F32),
                                        op0=ALU.mult, op1=ALU.subtract).then_inc(S["smlo"], 1)

            def w_rest(n, par):
                ve.wait_ge(S["whi"], done(n))
                ve.tensor_tensor(tile_of(w_lo, n), bank(2 * par, WCOLS),
                                 tile_of(w_hi, n).bitcast(F32),
                                 ALU.subtract).then_inc(S["wlo"], 1)

            for n in range(NSH):
                w_rest(n, n % 2)
            with ve.Fori(0, E // 2) as i:
                for k in range(2):
                    w_rest(NSH + 2 * i + k, k)

            def fill_lo(b, f):
                src_hi = (xT_hi, yT_hi, v_hi)[f // 2]
                dst = (xT_lo, yT_lo, v_lo)[f // 2]
                ve.wait_ge(S["fhi"], done(6 * b + f))
                c = slice(f % 2 * 512, f % 2 * 512 + 512)
                ve.tensor_tensor(dst[:, c], bank((7, 1)[f % 2]), src_hi[:, c].bitcast(F32), ALU.subtract).then_inc(S["flo"], 1)

            c_rinv = Chain(ve, S["c_rinv"], 1)

            def row_max(b, i):
                n = TB * b + i
                ve.wait_ge(S["score"], done(n))
                ve.wait_ge(S["prob"], done(TB * b - 1))
                ve.tensor_reduce(nmax[:, i:i + 1], bank(2 * (i % 2), (i + 1) * P), AXX, ALU.max,
                                 negate=True).then_inc(S["nmax"], 1)

            def pT_rest(b, i):
                ve.wait_ge(S["pThi"], done(TB * b + i))
                ve.tensor_tensor(pT_lo[i % 2][:, 0:(i + 1) * P], bank(4, (i + 1) * P),
                                 pT_hi[i % 2][:, 0:(i + 1) * P].bitcast(F32), ALU.subtract).then_inc(S["pTlo"], 1)

            def add_attn(b, i):
                n = TB * b + i
                c_rinv.start(n)
                ve.wait_ge(S["pv"], done(n))
                c_rinv.link(ve.reciprocal(rinv[:, i:i + 1], rsum[:, i:i + 1]))
                xt = tile_of(x_all, TB * b + i)
                ve.scalar_tensor_tensor(out=xt, in0=bank(6, P), scalar=rinv[:, i:i + 1], in1=xt,
                                        op0=ALU.mult, op1=ALU.add).then_inc(S["x2"], 1)

            def batch_dve(b, more):
                for i in range(TB):
                    row_max(b, i)
                    if i >= 1:
                        pT_rest(b, i - 1)
                    if i >= 2:
                        add_attn(b, i - 2)
                    if more and i == 4:
                        normalise(b + 1)
                if more:
                    fill_lo(b + 1, 0)
                    fill_lo(b + 1, 1)
                pT_rest(b, TB - 1)
                add_attn(b, TB - 2)
                if more:
                    fill_lo(b + 1, 2)
                    fill_lo(b + 1, 3)
                add_attn(b, TB - 1)
                if more:
                    fill_lo(b + 1, 4)
                    fill_lo(b + 1, 5)

            normalise(0)
            for f in range(6):
                fill_lo(0, f)
            with ve.Fori(0, B - 1) as b:
                batch_dve(b, True)
            batch_dve(B - 1, False)

            c_st2 = Chain(ve, S["c_st2"], 2 * GT)
            c_n2 = Chain(ve, S["c_n2"], GT)
            c_rt1 = Chain(ve, S["c_rt1"], 2 * GT + 4)
            c_rt2 = Chain(ve, S["c_rt2"], 11)

            def stats2(i, off):
                g = 2 * i + off
                c_st2.start(g)
                ve.wait_ge(S["x2"], done(NT - 1))
                for t in range(GT):
                    c_st2.inc(ve.bn_stats(stats[:, t, :], tile_of(x_all, g * GT + t)))
                c_st2.wait()
                alone(ve)
                for t in range(GT):
                    c_st2.inc(ve.bn_aggr(mv2[:, t, :], stats[:, t, :]))
                c_st2.end()
                ve.tensor_scalar(veps2[:], mv2[:, :, 1], EPS, None, ALU.add).then_inc(S["st2"], 1)

            def normalise2(i, off):
                g, par = 2 * i + off, off % 2
                ve.wait_ge(S["pow2"], done(g))
                c_n2.start(g)
                for t in range(GT):
                    c_n2.inc(ve.tensor_scalar(xrow[0][par][:, t, 0:C], tile_of(x_all, g * GT + t), mv2[:, t, 0:1],
                                              rstd2[:, t:t + 1], ALU.subtract, ALU.mult))
                c_n2.end()
                ve.nop().then_inc(S["norm2"], 1)

            def t2_lo(i, off):
                g = 2 * i + off
                ve.wait_ge(S["t2hi"], done(g))
                ve.tensor_tensor(x2T_lo[off % 2][:], bank(6), x2T_hi[off % 2][:].bitcast(F32),
                                 ALU.subtract).then_inc(S["t2lo"], 1)

            def route1(i, off):
                g = 2 * i + off
                c_rt1.start(g)
                ve.wait_ge(S["r3"], done(g))
                alone(ve)
                for t in range(GT):
                    c_rt1.inc(ve.max(top[:, t, :], bank(7, E, t * E)))
                c_rt1.wait()
                alone(ve)
                for t in range(GT):
                    c_rt1.inc(ve.max_index(topi[:, t, :], top[:, t, :], bank(7, E, t * E)))
                c_rt1.wait()
                c_rt1.link(ve.tensor_copy(topf[:], topi[:, :, 0:KTOP]))
                for k in range(KTOP):
                    c_rt1.inc(ve.tensor_tensor(hot[k][:], iota_e[:].unsqueeze(1).broadcast_to([P, GT, E]),
                                               topf[:, :, k:k + 1].broadcast_to([P, GT, E]), ALU.is_equal))
                c_rt1.inc(ve.tensor_tensor(gap[:], top[:, :, 0], top[:, :, 1], ALU.subtract))
                c_rt1.end()
                ve.tensor_tensor(hot_b[:], hot[0][:], hot[1][:], ALU.add).then_inc(S["rt1"], 1)

            def route2(i, off):
                g, par = 2 * i + off, off % 2
                c_rt2.start(g)
                ve.wait_ge(S["rk"], done(g))
                ve.wait_ge(S["tanh"], done(g))
                c_rt2.inc(ve.tensor_tensor(place[:], bank(7, GT * E, 64).rearrange("p (t e) -> p t e", e=E),
                                           count[:].unsqueeze(1).broadcast_to([P, GT, E]), ALU.add))
                c_rt2.link(ve.tensor_reduce(added[:], bank(7, GT * E, 128).rearrange("p (t e) -> p e t", e=E), AXX, ALU.add))
                c_rt2.inc(ve.tensor_tensor(count[:], count[:], added[:], ALU.add))
                for k in range(KTOP):
                    c_rt2.link(ve.tensor_tensor(picked[:], place[:], hot[k][:], ALU.mult))
                    c_rt2.link(ve.tensor_reduce(posf[:], picked[:], AXX, ALU.add))
                    c_rt2.link(ve.tensor_copy(pos[k][par][:], posf[:]))
                    c_rt2.inc(ve.tensor_scalar(xrow[k][par][:, :, C + 1], gapt[:], 0.5 - k, 0.5, ALU.mult, ALU.add))
                c_rt2.end()
                ve.nop().then_inc(S["rt2"], 1)

            def unit_mul(g, u):
                n = 4 * g + u
                ve.wait_ge(S["silu"], done(n))
                ve.wait_ge(S["hhi"], done(n - 2))
                ve.tensor_tensor(hid[u % 2][:], sil[u % 2][:], bank(2 * (u % 2) + 1), ALU.mult).then_inc(S["mul"], 1)

            def unit_lo(g, u):
                ve.wait_ge(S["hhi"], done(4 * g + u))
                ve.tensor_tensor(hT_lo[u % 2][:], hid[u % 2][:], hT_hi[u % 2][:].bitcast(F32),
                                 ALU.subtract).then_inc(S["hlo"], 1)

            def slot_tables():
                c = Chain(ve, S["c_tab"], 15)
                c.start(0)
                rows, tiles, ends = t8[0], t8[1], t8[2]
                c.inc(ve.tensor_scalar(padpos[:], count[:], part_id[:], None, ALU.add))
                c.link(ve.tensor_tensor(rows[:], count[0:1, :], region0[0:1, :], ALU.subtract))
                c.link(ve.tensor_scalar(t8i[:], rows[:], float(P - 1), None, ALU.add))
                c.link(ve.tensor_scalar(t8i[:], t8i[:], 7, None, ALU.arith_shift_right))
                c.link(ve.tensor_copy(tiles[:], t8i[:]))
                c.link(ve.tensor_tensor(t64[:], lower[:], tiles[:].unsqueeze(1).broadcast_to([1, E, E]), ALU.mult))
                c.link(ve.tensor_reduce(ends[:], t64[:], AXX, ALU.add))
                c.link(ve.tensor_tensor(past[:], iota_s[:].unsqueeze(2).broadcast_to([1, SLOTS, E]),
                                        ends[:].unsqueeze(1).broadcast_to([1, SLOTS, E]), ALU.is_ge))
                c.inc(ve.tensor_reduce(slot_e[:], past[:], AXX, ALU.add))
                c.link(ve.tensor_tensor(past2[:], past[:], tiles[:].unsqueeze(1).broadcast_to([1, SLOTS, E]), ALU.mult))
                c.link(ve.tensor_reduce(slot_t[:], past2[:], AXX, ALU.add))
                c.inc(ve.tensor_scalar(slot_wi[:], slot_e[:], float(E - 1), float(NSH), ALU.min, ALU.add))
                c.link(ve.tensor_tensor(slot_w[:], iota_s[:], slot_t[:], ALU.subtract))
                c.link(ve.tensor_scalar(slot_r[:], slot_w[:], float(P), None, ALU.mult))
                c.link(ve.scalar_tensor_tensor(out=slot_ri[:], in0=slot_e[:], scalar=float(REGION), in1=slot_r[:],
                                               op0=ALU.mult, op1=ALU.add))
                c.end()
                ve.nop().then_inc(S["tab"], 1)

            def add_shared(i, off):
                g = 2 * i + off
                ve.wait_ge(S["back"], done(g))
                xg4 = x_all[:, bass.ds(g * GT, GT), :]
                ve.tensor_tensor(xg4, xg4, bank(5).rearrange("p (t c) -> p t c", c=C), ALU.add).then_inc(S["addb"], 1)

            def shared_dve(i, off, more):
                g = 2 * i + off
                if more:
                    stats2(i, off + 1)
                unit_mul(g, 0)
                if more:
                    normalise2(i, off + 1)
                unit_mul(g, 1)
                unit_lo(g, 0)
                route2(i, off)
                unit_mul(g, 2)
                unit_lo(g, 1)
                if more:
                    t2_lo(i, off + 1)
                else:
                    slot_tables()
                unit_mul(g, 3)
                unit_lo(g, 2)
                unit_lo(g, 3)
                if more:
                    route1(i, off + 1)
                add_shared(i, off)

            ve.wait_ge(S["const"], 1)
            c_cnt = Chain(ve, S["c_cnt"], 1)
            c_cnt.start(0)
            c_cnt.link(ve.tensor_copy(count[:], region0[:]))
            stats2(0, 0)
            normalise2(0, 0)
            t2_lo(0, 0)
            route1(0, 0)
            with ve.Fori(0, NG // 2 - 1) as i:
                shared_dve(i, 0, True)
                shared_dve(i, 1, True)
            shared_dve(NG // 2 - 1, 0, True)
            shared_dve(NG // 2 - 1, 1, False)

            def x_lo(i, off):
                p, par = 2 * i + off, off % 2
                for k in range(2):
                    ve.wait_ge(s_xg[2 * par + k], (i + off // 2 + 1) * 16)
                ve.tensor_copy(meta[:, bass.ds(2 * p, 2), :], xg[:, 2 * par:2 * par + 2, C:C + 2]).then_inc(S["emeta"], 1)
                ve.wait_ge(S["xhi"], done(p))
                ve.tensor_tensor(gT_lo[par][:], bank(4, 2 * P), gT_hi[par][:].bitcast(F32), ALU.subtract).then_inc(S["xlo"], 1)

            def e_mul(i, off):
                p, par = 2 * i + off, off % 2
                ve.wait_ge(S["esilu"], done(p))
                ve.wait_ge(S["eth"], done(p - 2))
                ve.tensor_tensor(hid[par][:].rearrange("p (s h) -> p s h", s=2), sil[par][:].rearrange("p (s h) -> p s h", s=2),
                                 halves(ps[:, 1024 * par:1024 * par + 1024], 1), ALU.mult).then_inc(S["emul"], 1)

            def h_lo(i, off):
                p, par = 2 * i + off, off % 2
                ve.wait_ge(S["ehhi"], done(p))
                ve.tensor_tensor(hT_lo[par][:], bank(5), hT_hi[par][:].bitcast(F32), ALU.subtract).then_inc(S["ehlo"], 1)

            def y_out(i, off):
                p, par = 2 * i + off, off % 2
                ve.wait_ge(S["ey"], done(p))
                ve.wait_ge(S["ysent"], done(p - 2))
                ve.wait_ge(S["emeta"], done(p))
                for k in range(2):
                    ve.tensor_scalar(yrow[2 * par + k][:], bank(6, P, k * P),
                                     meta[:, bass.ds(2 * p + k, 1), 1], None, ALU.mult).then_inc(S["eyout"], 1)

            def e_step(i, off, x=True, h=True, y=True):
                if x:
                    x_lo(i, off + 2)
                if h:
                    e_mul(i, off + 1)
                h_lo(i, off)
                if y:
                    y_out(i, off - 1)

            x_lo(0, 0)
            x_lo(0, 1)
            e_mul(0, 0)
            e_step(0, 0, y=False)
            with ve.Fori(0, PAIRS // 2 - 2) as i:
                e_step(i, 1)
                e_step(i, 2)
            L = PAIRS // 2 - 1
            e_step(L - 1, 1)
            e_step(L, 0, x=False)
            e_step(L, 1, x=False, h=False)
            y_out(L, 1)

            for n in range(NC):
                ve.wait_ge(S["fin0"], done(n))
                xc = x_all[:, n * CT:(n + 1) * CT, :]
                ve.tensor_tensor(xc, xc, yb[0][n % 2], ALU.add).then_inc(S["fin"], 1)

        @block.tensor
        def _(pe):
            credit(pe, "wT", "smT", "score", "pT", "pv", "fill", "t2", "lt", "r3", "rk", "gu", "yT", "back",
                   "tx", "eh", "eth", "ey")

            def product(dst, a_hi, a_lo, b_hi, b_lo, start=True, stop=True):
                pe.matmul(dst, a_lo, b_hi, start=start, stop=False)
                pe.matmul(dst, a_hi, b_lo, start=False, stop=False)
                return pe.matmul(dst, a_hi, b_hi, start=False, stop=stop)

            pe.wait_ge(S["const"], 1)
            pe.wait_ge(s_small, 5 * 16)
            pe.transpose(bank(7, P), wqkv[:, 2, :], ident[:])
            pe.matmul(bank(7, P, P), wqkv[:, 0, :], wqkv[:, 1, :], start=True, stop=True)
            pe.transpose(bank(7, P, 2 * P), rw_raw[:], ident[:]).then_inc(S["smT"], 1)
            wv_hi, wv_lo = sm_hi[:, 0:C], sm_lo[:, 0:C]
            m_hi, m_lo = sm_hi[:, C:2 * C], sm_lo[:, C:2 * C]
            r_hi, r_lo = sm_hi[:, 2 * C:SM], sm_lo[:, 2 * C:SM]

            def w_transpose(n, par, count):
                pe.wait_ge(s_raw[par], count)
                pe.wait_ge(S["wlo"], done(n - 2))
                for j in range(WBLK):
                    last = pe.transpose(bank(2 * par, P, j * P), raw[par][:, j, :], ident[:])
                last.then_inc(S["wT"], 1)

            for n in range(NSH):
                w_transpose(n, n % 2, 3 * 16)
            with pe.Fori(0, E // 2) as i:
                for k in range(2):
                    w_transpose(NSH + 2 * i + k, k, (i + 2) * 3 * 16)

            def fill(b, f):
                dst = bank((7, 1)[f % 2])
                pe.wait_ge(S["flo"], done(6 * b + f - 2))
                if f < 2:
                    if f == 0:
                        pe.wait_ge(S["norm1"], done(TB * b + TB - 1))
                    for j in range(4):
                        last = pe.transpose(dst[:, j * P:(j + 1) * P], xn[:, 4 * f + j, :], ident[:])
                elif f < 4:
                    c = slice(f % 2 * 512, f % 2 * 512 + 512)
                    last = product(dst, m_hi, m_lo, xT_hi[:, c], xT_lo[:, c])
                else:
                    for j in range(4):
                        c = slice((f % 2 * 4 + j) * P, (f % 2 * 4 + j + 1) * P)
                        last = product(dst[:, j * P:(j + 1) * P], xT_hi[:, c], xT_lo[:, c], wv_hi, wv_lo)
                last.then_inc(S["fill"], 1)

            def score(b, i):
                n = TB * b + i
                pe.wait_ge(S["prob"], done(n - 2))
                q = slice(i * P, (i + 1) * P)
                width = (i + 1) * P
                base = 2 * (i % 2)
                for c0 in range(0, width, 512):
                    c1 = min(c0 + 512, width)
                    product(bank(base, c1 - c0, c0), yT_hi[:, q], yT_lo[:, q], xT_hi[:, c0:c1], xT_lo[:, c0:c1],
                            stop=c1 < width)
                pe.matmul(bank(base, P, i * P), ident_b[:], mask_b[:], start=False, stop=True).then_inc(S["score"], 1)

            def p_transpose(b, i):
                n = TB * b + i
                pe.wait_ge(S["prob"], done(n))
                pe.wait_ge(S["pTlo"], done(n - 1))
                for j in range(i + 1):
                    last = pe.transpose(bank(4, P, j * P), prob[i % 2][:, j * P:(j + 1) * P], ident[:])
                last.then_inc(S["pT"], 1)

            def pv(b, i):
                n = TB * b + i
                pe.wait_ge(S["pTlo"], done(n))
                pe.wait_ge(S["x2"], done(n - 1))
                dst = bank(6, P)
                for j in range(i + 1):
                    c = slice(j * P, (j + 1) * P)
                    last = product(dst, pT_hi[i % 2][:, c], pT_lo[i % 2][:, c], v_hi[:, c], v_lo[:, c],
                                   start=j == 0, stop=j == i)
                last.then_inc(S["pv"], 1)

            def batch_pe(b, more):
                for i in range(TB):
                    score(b, i)
                    if i == 0:
                        pe.wait_ge(S["flo"], done(6 * b + 5))
                    if i >= 2:
                        pv(b, i - 2)
                    if i >= 1:
                        p_transpose(b, i - 1)
                if more:
                    pe.wait_ge(S["prob"], done(TB * b + 6))
                    fill(b + 1, 0)
                    fill(b + 1, 1)
                pv(b, TB - 2)
                p_transpose(b, TB - 1)
                if more:
                    fill(b + 1, 2)
                    fill(b + 1, 3)
                pv(b, TB - 1)
                if more:
                    fill(b + 1, 4)
                    fill(b + 1, 5)

            pe.wait_ge(S["smlo"], done(2))
            pe.wait_ge(S["wlo"], done(NX - 1))
            for f in range(6):
                fill(0, f)
            with pe.Fori(0, B - 1) as b:
                batch_pe(b, True)
            batch_pe(B - 1, False)

            def t2(i, off):
                g, par = 2 * i + off, off % 2
                pe.wait_ge(S["norm2"], done(g))
                pe.wait_ge(S["lthi"], done(g - 1))
                for t in range(GT):
                    last = pe.transpose(bank(6, P, t * P), xrow[0][par][:, t, 0:C], ident[:])
                last.then_inc(S["t2"], 1)

            def logits_T(i, off):
                g = 2 * i + off
                pe.wait_ge(S["t2lo"], done(g))
                product(bank(6), r_hi, r_lo, x2T_hi[off % 2][:], x2T_lo[off % 2][:]).then_inc(S["lt"], 1)

            def logits(i, off):
                g = 2 * i + off
                pe.wait_ge(S["lthi"], done(g))
                pe.wait_ge(S["rt2"], done(g - 1))
                alone(pe)
                for t in range(GT):
                    last = pe.transpose(bank(7, E, t * E), logitT[:, t * P:(t + 1) * P], ident[0:E, 0:E])
                last.then_inc(S["r3"], 1)

            def ranks(i, off):
                g = 2 * i + off
                pe.wait_ge(S["rt1"], done(g))
                pe.wait_ge(S["rt2"], done(g - 1))
                hot2 = hot_b[:].rearrange("p t e -> p (t e)")
                pe.matmul(bank(7, GT * E, 64), upper_b[:], hot2, start=True, stop=False)
                for t in range(GT - 1):
                    pe.matmul(bank(7, (GT - 1 - t) * E, 64 + (t + 1) * E).rearrange("p (t e) -> p t e", e=E), ones_b[:],
                              hot_b[:, t:t + 1, :].broadcast_to([P, GT - 1 - t, E]), start=False, stop=t == GT - 2)
                pe.matmul(bank(7, GT * E, 128), ones_b[:], hot2, start=True, stop=True).then_inc(S["rk"], 1)

            def unit_up(i, off, u):
                g = 2 * i + off
                pe.wait_ge(S["mul"], done(4 * g + u - 2))
                xs, j = u // 2, u % 2
                for n in range(2):
                    c = slice((2 * n + j) * P, (2 * n + j + 1) * P)
                    last = product(bank(2 * (u % 2) + n), w_hi[:, xs, c], w_lo[:, xs, c], x2T_hi[off % 2][:], x2T_lo[off % 2][:])
                last.then_inc(S["gu"], 1)

            def unit_down(i, off, u):
                g = 2 * i + off
                xs, j = u // 2, u % 2
                c = slice((4 + j) * P, (5 + j) * P)
                pe.wait_ge(S["hlo"], done(4 * g + u))
                if u == 0:
                    pe.wait_ge(S["yThi"], done(g - 1))
                product(bank(4), w_hi[:, xs, c], w_lo[:, xs, c], hT_hi[u % 2][:], hT_lo[u % 2][:],
                        start=u == 0, stop=u == 3).then_inc(S["yT"], 1)

            def shared_back(i, off):
                g = 2 * i + off
                pe.wait_ge(S["yThi"], done(g))
                pe.wait_ge(S["addb"], done(g - 1))
                for t in range(GT):
                    last = pe.transpose(bank(5, P, t * P), shT[:, t * P:(t + 1) * P], ident[:])
                last.then_inc(S["back"], 1)

            def shared_pe(i, off, more):
                unit_up(i, off, 0)
                unit_up(i, off, 1)
                ranks(i, off)
                unit_down(i, off, 0)
                unit_up(i, off, 2)
                unit_down(i, off, 1)
                if more:
                    t2(i, off + 1)
                unit_up(i, off, 3)
                unit_down(i, off, 2)
                if more:
                    logits_T(i, off + 1)
                unit_down(i, off, 3)
                if more:
                    logits(i, off + 1)
                shared_back(i, off)

            pe.wait_ge(S["x2"], done(NT - 1))
            t2(0, 0)
            logits_T(0, 0)
            logits(0, 0)
            with pe.Fori(0, NG // 2 - 1) as i:
                shared_pe(i, 0, True)
                shared_pe(i, 1, True)
            shared_pe(NG // 2 - 1, 0, True)
            shared_pe(NG // 2 - 1, 1, False)

            def slot_expert(p, k):
                return pe.value_load(slot_wi[0:1, bass.ds(2 * p + k, 1)], min_val=NSH, max_val=NX - 1)

            def x_transpose(i, off):
                p, par = 2 * i + off, off % 2
                for k in range(2):
                    pe.wait_ge(s_xg[2 * par + k], (i + off // 2 + 1) * 16)
                pe.wait_ge(S["xlo"], done(p - 1))
                for k in range(2):
                    last = pe.transpose(bank(4, P, k * P), xg[:, 2 * par + k, 0:C], ident[:])
                last.then_inc(S["tx"], 1)

            def up(i, off):
                p, par = 2 * i + off, off % 2
                pe.wait_ge(S["xlo"], done(p))
                pe.wait_ge(S["emul"], done(p - 2))
                for k in range(2):
                    e = bass.ds(slot_expert(p, k), 1)
                    c = slice(k * P, (k + 1) * P)
                    last = product(bank(2 * par + k), gT_hi[par][:, c], gT_lo[par][:, c],
                                   w_hi[:, e, 0:2 * HID].rearrange("p o c -> p (o c)"),
                                   w_lo[:, e, 0:2 * HID].rearrange("p o c -> p (o c)"))
                last.then_inc(S["eh"], 1)

            def h_transpose(i, off):
                p, par = 2 * i + off, off % 2
                pe.wait_ge(S["emul"], done(p))
                pe.wait_ge(S["ehlo"], done(p - 1))
                for j in range(4):
                    last = pe.transpose(bank(5, P, j * P), hid[par][:, j * P:(j + 1) * P], ident[:])
                last.then_inc(S["eth"], 1)

            def down(i, off):
                p, par = 2 * i + off, off % 2
                pe.wait_ge(S["ehlo"], done(p))
                pe.wait_ge(S["eyout"], done(2 * p - 1))
                for k in range(2):
                    e = bass.ds(slot_expert(p, k), 1)
                    for j in range(2):
                        c = slice((2 * k + j) * P, (2 * k + j + 1) * P)
                        o = 2 * HID + j * C
                        last = product(bank(6, P, k * P), hT_hi[par][:, c], hT_lo[par][:, c],
                                       w_hi[:, e, o:o + C].rearrange("p o c -> p (o c)"),
                                       w_lo[:, e, o:o + C].rearrange("p o c -> p (o c)"), start=j == 0, stop=j == 1)
                last.then_inc(S["ey"], 1)

            def e_step(i, off, x=True, h=True, y=True):
                if x:
                    x_transpose(i, off + 2)
                if h:
                    up(i, off + 1)
                h_transpose(i, off)
                if y:
                    down(i, off - 1)

            pe.wait_ge(S["tab"], 1)
            pe.wait_ge(S["addb"], done(NG - 1))
            x_transpose(0, 0)
            x_transpose(0, 1)
            up(0, 0)
            e_step(0, 0, y=False)
            with pe.Fori(0, PAIRS // 2 - 2) as i:
                e_step(i, 1)
                e_step(i, 2)
            L = PAIRS // 2 - 1
            e_step(L - 1, 1)
            e_step(L, 0, x=False)
            e_step(L, 1, x=False, h=False)
            down(L, 1)


INPUTS = ["L0_attn_x", "L0_attn_Wk", "L0_attn_Wq", "L0_attn_Wv", "L0_ffn_router_w", "L0_ffn_expert_bias",
          "L0_ffn_w1", "L0_ffn_w3", "L0_ffn_w2", "L0_ffn_sw1", "L0_ffn_sw3", "L0_ffn_sw2"]


def kernel(**inputs):
    import numpy as np
    import concourse.bacc as bacc
    from concourse.bass_utils import run_bass_kernel_spmd

    nc = bacc.Bacc("TRN2", target_bir_lowering=False, num_devices=1)
    arrays, args = {}, []
    for name in INPUTS:
        a = np.ascontiguousarray(inputs[name])
        arrays[name] = a
        args.append(nc.dram_tensor(name, a.shape, mybir.dt.from_np(a.dtype), kind="ExternalInput").ap())
    shape = arrays["L0_attn_x"].shape
    tokens, experts = shape[0] * shape[1], arrays["L0_ffn_w1"].shape[0]
    out = nc.dram_tensor("out", shape, F32, kind="ExternalOutput").ap()
    xbuf = nc.dram_tensor("xbuf", (experts * (tokens + P) + 8 * P, shape[2] + 2), F32).ap()
    ybuf = nc.dram_tensor("ybuf", (2 * tokens, shape[2]), F32).ap()
    build(nc, *args, out, xbuf, ybuf)
    r = run_bass_kernel_spmd(nc, [arrays], core_ids=[0])
    return r.results[0]["out"]
```

```python
from contextlib import ExitStack

import concourse.bass as bass
from concourse import mybir

F32 = mybir.dt.float32
F32R = mybir.dt.float32r
BF16 = mybir.dt.bfloat16
I32 = mybir.dt.int32
U32 = mybir.dt.uint32
ALU = mybir.AluOpType
ACT = mybir.ActivationFunctionType
AXX = mybir.AxisListType.X

P = 128
CREDIT = 3
EPS = 1e-5
MASKED = -3.0e38


def done(n):
    return n + 1 + CREDIT


class Chain:

    def __init__(self, eng, sem, per):
        self.eng, self.sem, self.per = eng, sem, per

    def start(self, n):
        self.base, self.k = CREDIT + n * self.per, 0

    def inc(self, ins):
        self.k += 1
        ins.then_inc(self.sem, 1)

    def link(self, ins):
        self.inc(ins)
        self.wait()

    def wait(self):
        self.eng.wait_ge(self.sem, self.base + self.k)

    def end(self):
        self.wait()
        assert self.k == self.per, self.k


def build(nc, x, wk, wq, wv, router_w, expert_bias, w1, w3, w2, sw1, sw3, sw2, out, xbuf, ybuf):
    B, T, C = x.shape
    E, HID, _ = w1.shape
    NSH = sw1.shape[0]
    NX = NSH + E
    NTOK = B * T
    NT = NTOK // P
    TB = T // P
    KTOP = 2
    REGION = NTOK + P
    ROW = C + 2
    SLOTS = 4 * -(-((KTOP * NTOK + E * (P - 1)) // P) // 4)
    PAIRS = SLOTS // 2
    SPARE = SLOTS - KTOP * NTOK // P
    GT = 4
    NG = NT // GT
    WCOLS = 2 * HID + HID // P * C
    WBLK = WCOLS // P
    SCALE = float(C) ** -0.5
    assert C == P and HID == 2 * P and SPARE <= 8

    x_rows = x.rearrange("b (t p) c -> p (b t) c", p=P)
    out_rows = out.rearrange("b (t p) c -> p (b t) c", p=P)

    with ExitStack() as ctx:
        def sb(name, shape, dt=F32):
            return ctx.enter_context(nc.sbuf_tensor(name, shape, dt))

        def sem(name):
            return ctx.enter_context(nc.semaphore(name))

        x_all = sb("x_all", [P, NT, C])
        w_hi = sb("w_hi", [P, NX, WCOLS], F32R)
        w_lo = sb("w_lo", [P, NX, WCOLS], F32R)
        raw = [sb(f"raw{n}", [P, WBLK, P]) for n in range(2)]
        wqkv = sb("wqkv", [P, 3, C])
        rw_raw = sb("rw_raw", [P, C])
        bias_col = sb("bias_col", [E, 1])
        SM = 3 * C
        sm_hi = sb("sm_hi", [P, SM], F32R)
        sm_lo = sb("sm_lo", [P, SM], F32R)
        ident = sb("ident", [P, P])
        ident_b = sb("ident_b", [P, P], BF16)
        ones_b = sb("ones_b", [P, P], BF16)
        upper_b = sb("upper_b", [P, P], BF16)
        mask_b = sb("mask_b", [P, P], BF16)
        mhalf = sb("mhalf", [P, TB])
        iota_e = sb("iota_e", [P, E])
        region0 = sb("region0", [P, E])
        padrow = sb("padrow", [P, ROW])
        row_id = sb("row_id", [P, KTOP, NT], I32)

        stats = sb("stats", [P, TB, 6])
        mv = sb("mv", [P, TB, 2])
        veps = sb("veps", [P, TB])
        rstd = sb("rstd", [P, TB])
        xn = sb("xn", [P, TB, C])
        xT_hi = sb("xT_hi", [P, T], F32R)
        xT_lo = sb("xT_lo", [P, T], F32R)
        yT_hi = sb("yT_hi", [P, T], F32R)
        yT_lo = sb("yT_lo", [P, T], F32R)
        v_hi = sb("v_hi", [P, T], F32R)
        v_lo = sb("v_lo", [P, T], F32R)
        prob = [sb(f"prob{n}", [P, T]) for n in range(2)]
        pT_hi = [sb(f"pT_hi{n}", [P, T], F32R) for n in range(2)]
        pT_lo = [sb(f"pT_lo{n}", [P, T], F32R) for n in range(2)]
        nmax = sb("nmax", [P, TB])
        rsum = sb("rsum", [P, TB])
        rinv = sb("rinv", [P, TB])

        stats2 = sb("stats2", [P, TB, 6])
        mv2 = sb("mv2", [P, TB, 2])
        veps2 = sb("veps2", [P, NT])
        mean2 = sb("mean2", [P, NT])
        rstd2 = sb("rstd2", [P, NT])
        shift2 = sb("shift2", [P, NT])
        xrow = [[sb(f"xrow{k}{n}", [P, GT, ROW]) for n in range(2)] for k in range(KTOP)]
        x2T_hi = [sb(f"x2T_hi{n}", [P, GT * P], F32R) for n in range(2)]
        x2T_lo = [sb(f"x2T_lo{n}", [P, GT * P], F32R) for n in range(2)]
        logitT = sb("logitT", [E, GT * P])
        logit = sb("logit", [P, GT, E])
        top = sb("top", [P, GT, 8])
        topi = sb("topi", [P, GT, 8], U32)
        topf = sb("topf", [P, KTOP, GT])
        hot = sb("hot", [P, KTOP, GT, E])
        hot_b = sb("hot_b", [P, GT, E], BF16)
        gap = sb("gap", [P, GT])
        gapt = sb("gapt", [P, GT])
        count = sb("count", [P, E])
        added = sb("added", [P, E])
        place = sb("place", [P, GT, E])
        picked = sb("picked", [P, KTOP, GT, E])
        posf = sb("posf", [P, KTOP, GT])
        pos = [sb(f"pos{n}", [P, KTOP, GT], I32) for n in range(2)]
        sil = [sb(f"sil{n}", [P, 512]) for n in range(2)]
        hid = [sb(f"hid{n}", [P, 512]) for n in range(2)]
        hT_hi = [sb(f"hT_hi{n}", [P, 512], F32R) for n in range(2)]
        hT_lo = [sb(f"hT_lo{n}", [P, 512], F32R) for n in range(2)]
        shT = sb("shT", [P, GT * P])

        padpos = sb("padpos", [1, E], I32)
        t8 = [sb(f"t8_{n}", [1, E]) for n in range(5)]
        t8i = sb("t8i", [1, E], I32)
        lower = sb("lower", [1, E, E])
        t64 = sb("t64", [1, E, E])
        iota_s = sb("iota_s", [1, SLOTS])
        past = sb("past", [1, SLOTS, E])
        past2 = sb("past2", [1, SLOTS, E])
        slot_e = sb("slot_e", [1, SLOTS])
        slot_t = sb("slot_t", [1, SLOTS])
        slot_w = sb("slot_w", [1, SLOTS])
        slot_r = sb("slot_r", [1, SLOTS])
        pair_w = sb("pair_w", [1, PAIRS])
        step_w = sb("step_w", [1, PAIRS + 3])
        step_wi = sb("step_wi", [1, PAIRS + 3], I32)
        slot_ri = sb("slot_ri", [1, SLOTS], I32)
        xg = sb("xg", [P, 4, ROW])
        meta = sb("meta", [P, SLOTS, 2])
        gT_hi = [sb(f"gT_hi{n}", [P, 2 * P], F32R) for n in range(2)]
        gT_lo = [sb(f"gT_lo{n}", [P, 2 * P], F32R) for n in range(2)]
        yrow = [sb(f"yrow{n}", [P, C]) for n in range(4)]
        yid = [sb(f"yid{n}", [P, 1], I32) for n in range(4)]
        NC = 8
        CT = NT // NC
        RING = 4
        yb11 = sb("yb11", [P, T])
        parts = [a[:, h * CT * C:(h + 1) * CT * C].rearrange("p (t c) -> p t c", c=C)
                 for a in (prob[0][:], prob[1][:], xn[:].rearrange("p t c -> p (t c)"), yb11[:]) for h in range(2)]
        yb = [parts[0:RING], parts[RING:2 * RING]]

        ps = ctx.enter_context(nc.psum_tensor("ps", [P, 8 * 512], F32))

        def bank(n, cols=512, first=0):
            return ps[:, n * 512 + first:n * 512 + first + cols]

        def tile_of(a, t):
            return a[:, bass.ds(t, 1), :].rearrange("p o c -> p (o c)")

        WHALF = WCOLS // 2

        def w_halves(a, b, j):
            return a[:, bass.ds(NSH + 2 * b + j // 2, 1), j % 2 * WHALF:(j % 2 + 1) * WHALF].rearrange("p o c -> p (o c)")

        ORDER = [n // 2 if n % 2 == 0 else TB - 1 - n // 2 for n in range(TB)]

        def chunks(k):
            i = ORDER[k]
            if k % 2 == 0:
                return [(1, 0, i + 1)]
            return [(4, 0, 4), (5, 4, i + 1)]

        CH = [sum(len(chunks(m)) for m in range(k)) for k in range(TB)]
        NCH = CH[-1] + len(chunks(TB - 1))

        def halves(a, k):
            return a.rearrange("p (s h) -> p s h", s=2)[:, :, k * HID:(k + 1) * HID]

        def alone(eng):
            eng.sem_inc(S["passed"], 1)

        s_x0 = sem("s_x0")
        s_x1 = sem("s_x1")
        s_small = sem("s_small")
        s_raw = [sem(f"s_raw{n}") for n in range(2)]
        s_pad0 = sem("s_pad0")
        s_rows = [sem(f"s_rows{n}") for n in range(2)]
        s_padw = sem("s_padw")
        s_xg = [sem(f"s_xg{n}") for n in range(4)]
        s_yw = [sem(f"s_yw{n}") for n in range(4)]
        s_yb = [sem(f"s_yb{n}") for n in range(NC)]
        s_out = [sem(f"s_out{n}") for n in range(2)]
        names = ("c_fin row1 wfT wfhi wflo c_const c_norm2 c_yid c_st1 rinv c_st2 c_rt1 c_rt2 c_tab c_cnt c_n2 zeroed pow1 pow2 passed const wT whi wlo smT smhi smlo st1 norm1 score nmax prob pT pThi pTlo pv x2 "
                 "fill fhi flo st2 norm2 shift2 t2 t2hi t2lo lt lthi r3 rt1 rk rt2 tanh rows_sent "
                 "gu silu mul hhi hlo yT yThi back addb tab routed tx xhi xlo emeta eh esilu emul eth ehhi ehlo ey eyout "
                 "ysent yall fin0 fin").split()
        S = {n: sem("s_" + n) for n in names}

        block = ctx.enter_context(nc.Block())

        def credit(eng, *which):
            for n in which:
                eng.sem_inc(S[n], CREDIT)

        @block.sync
        def _(sp):
            sp.dma_start(x_all[:, 0:TB, :], x_rows[:, 0:TB, :]).then_inc(s_x0, 16)
            for n, w in enumerate((wq, wk, wv)):
                sp.dma_start(wqkv[:, n, :], w).then_inc(s_small, 16)
            sp.wait_ge(S["zeroed"], 1)
            sp.dma_start(rw_raw[0:E, :], router_w).then_inc(s_small, 16)
            sp.dma_start(bias_col[:], expert_bias.rearrange("(e o) -> e o", o=1)).then_inc(s_small, 16)

            def load_expert(par, a1, a3, a2):
                sp.dma_start(raw[par][:, 0:2, :], a1.rearrange("o (j p) c -> p (o j) c", p=P)).then_inc(s_raw[par], 16)
                sp.dma_start(raw[par][:, 2:4, :], a3.rearrange("o (j p) c -> p (o j) c", p=P)).then_inc(s_raw[par], 16)
                sp.dma_start(raw[par][:, 4:6, :].rearrange("p j c -> p (j c)"),
                             a2.rearrange("o p h -> p (o h)")).then_inc(s_raw[par], 16)

            for n in range(NSH):
                load_expert(n, sw1[n:n + 1], sw3[n:n + 1], sw2[n:n + 1])
            sp.dma_start(x_all[:, TB:NT, :], x_rows[:, TB:NT, :]).then_inc(s_x1, 16)
            with sp.Fori(0, B) as b:
                for k in range(2):
                    sp.wait_ge(S["wT"], done(2 * b + k))
                    e = bass.ds(2 * b + k, 1)
                    load_expert(k, w1[e, :, :], w3[e, :, :], w2[e, :, :])
            sp.wait_ge(S["const"], 1)
            for n in range(8):
                r = E * REGION + n * P
                sp.dma_start(xbuf[r:r + P, :], padrow[:]).then_inc(s_pad0, 16)

            sp.wait_ge(s_pad0, 8 * 16)
            sp.wait_ge(S["tab"], 1)
            for e in range(E):
                r = sp.value_load(padpos[0:1, e:e + 1], min_val=0, max_val=E * REGION - P)
                sp.dma_start(xbuf[bass.ds(r, P), :], padrow[:]).then_inc(s_padw, 16)
            sp.wait_ge(s_padw, E * 16)
            sp.wait_ge(S["routed"], 1)

            def load_slots(i, off):
                p, par = 2 * i + off, off % 2
                sp.wait_ge(S["tx"], done(p - 2))
                sp.wait_ge(S["emeta"], done(p - 2))
                for k in range(2):
                    r = sp.value_load(slot_ri[0:1, bass.ds(2 * p + k, 1)], min_val=0, max_val=E * REGION + 7 * P)
                    q = 2 * par + k
                    sp.dma_start(xg[:, q, :], xbuf[bass.ds(r, P), :]).then_inc(s_xg[q], 16)

            with sp.Fori(0, PAIRS // 2) as i:
                load_slots(i, 0)
                load_slots(i, 1)

            sp.wait_ge(S["yall"], 1)
            for n in range(NC):
                if n >= RING:
                    sp.wait_ge(S["fin"], done(n - RING))
                for k in range(KTOP):
                    src = ybuf[k * NTOK + n * CT * P:k * NTOK + (n + 1) * CT * P, :]
                    sp.dma_start(yb[k][n % RING], src.rearrange("(t p) c -> p t c", p=P)).then_inc(s_yb[n], 16)
            for h in range(2):
                sp.wait_ge(s_out[h], NC // 2 * 16)

        @block.gpsimd
        def _(pl):
            credit(pl, "c_const", "c_norm2", "c_yid", "pow1", "pow2", "ysent", "rows_sent")

            pl.memset(rw_raw[:], 0.0).then_inc(S["zeroed"], 1)
            cc = Chain(pl, S["c_const"], 0)
            cc.start(0)
            for a, value in ((ident, 0.0), (ident_b, 0.0), (ones_b, 1.0), (upper_b, 0.0), (mask_b, 0.0), (mhalf, -0.5),
                             (lower, 1.0), (padrow, 0.0)):
                cc.inc(pl.memset(a[:], value))
            for a, pattern, per_part in ((iota_e, [[1, E]], 0), (region0, [[REGION, E]], 0), (iota_s, [[1, SLOTS]], 0), (row_id, [[NTOK, KTOP], [P, NT]], 1)):
                cc.inc(pl.iota(a[:], pattern=pattern, base=0, channel_multiplier=per_part,
                               allow_small_or_imprecise_dtypes=True))
            cc.wait()
            for a in (ident, ident_b):
                cc.inc(pl.affine_select(out=a[:], in_=a[:], compare_op=ALU.not_equal, fill=1.0, base=0,
                                        pattern=[[-1, P]], channel_multiplier=1))
            for a, fill in ((upper_b, 1.0), (mask_b, MASKED)):
                cc.inc(pl.affine_select(out=a[:], in_=a[:], compare_op=ALU.is_ge, fill=fill, base=0,
                                        pattern=[[-1, P]], channel_multiplier=1))
            cc.inc(pl.affine_select(out=lower[:], in_=lower[:], compare_op=ALU.is_ge, fill=0.0, base=0,
                                    pattern=[[1, E], [-1, E]], channel_multiplier=0))
            cc.inc(pl.iota(padrow[:, C:C + 1].bitcast(I32), pattern=[[0, 1]], base=KTOP * NTOK, channel_multiplier=0))
            cc.wait()
            pl.nop().then_inc(S["const"], 1)

            def rstd_1():
                pl.tensor_tensor(rstd[:], veps[:], mhalf[:], ALU.pow).then_inc(S["pow1"], 1)

            def rstd_2(b):
                pl.wait_ge(S["st2"], done(b))
                alone(pl)
                bt = bass.ds(b * TB, TB)
                pl.tensor_tensor(rstd2[:, bt], veps2[:, bt], mhalf[:], ALU.pow).then_inc(S["pow2"], 1)

            pl.wait_ge(S["st1"], done(0))
            rstd_1()
            with pl.Fori(0, B - 1) as b:
                pl.wait_ge(S["st1"], done(b + 1))
                rstd_1()
                rstd_2(b)
            rstd_2(B - 1)

            c2 = Chain(pl, S["c_norm2"], KTOP)

            def row_names(i, off):
                g, par = 2 * i + off, off % 2
                c2.start(g)
                for k in range(KTOP):
                    c2.inc(pl.tensor_copy(xrow[k][par][:, :, C].bitcast(I32), row_id[:, k, bass.ds(g * GT, GT)]))
                c2.end()

            def send(i, off):
                g, par = 2 * i + off, off % 2
                pl.wait_ge(S["row1"], done(KTOP * g + 1))
                pl.wait_ge(S["rt2"], done(g))
                alone(pl)
                for t in range(GT):
                    for k in range(KTOP):
                        pl.indirect_dma_start(
                            out=xbuf, out_offset=bass.IndirectOffsetOnAxis(ap=pos[par][:, k, t:t + 1], axis=0),
                            in_=xrow[k][par][:, t, :], in_offset=None).then_inc(s_rows[par], 16)

            def sent(i, off):
                pl.wait_ge(s_rows[off % 2], (i + off // 2 + 1) * GT * KTOP * 16)
                alone(pl)
                pl.sem_inc(S["rows_sent"], 1)

            row_names(0, 0)
            row_names(0, 1)
            send(0, 0)
            send(0, 1)
            with pl.Fori(0, NG // 2 - 1) as i:
                for off in range(2):
                    sent(i, off)
                    row_names(i, off + 2)
                    send(i, off + 2)
            sent(NG // 2 - 1, 0)
            sent(NG // 2 - 1, 1)
            pl.nop().then_inc(S["routed"], 1)


            c3 = Chain(pl, S["c_yid"], 2)

            def send_y(i, off):
                p, par = 2 * i + off, off % 2
                c3.start(p)
                pl.wait_ge(S["emeta"], done(p))
                for k in range(2):
                    c3.inc(pl.tensor_copy(yid[2 * par + k][:], meta[:, bass.ds(2 * p + k, 1), 0].bitcast(I32)))
                c3.end()
                for k in range(2):
                    q = 2 * par + k
                    pl.wait_ge(S["eyout"], done(2 * p + k))
                    alone(pl)
                    pl.indirect_dma_start(out=ybuf, out_offset=bass.IndirectOffsetOnAxis(ap=yid[q][:], axis=0),
                                          in_=yrow[q][:], in_offset=None, bounds_check=KTOP * NTOK - 1,
                                          oob_is_err=False).then_inc(s_yw[q], 16)

            def sent_y(i, off):
                for k in range(2):
                    pl.wait_ge(s_yw[2 * (off % 2) + k], (i + off // 2 + 1) * 16)
                pl.nop().then_inc(S["ysent"], 1)

            send_y(0, 0)
            with pl.Fori(0, PAIRS // 2 - 1) as i:
                send_y(i, 1)
                sent_y(i, 0)
                send_y(i, 2)
                sent_y(i, 1)
            send_y(PAIRS // 2 - 1, 1)
            sent_y(PAIRS // 2 - 1, 0)
            sent_y(PAIRS // 2 - 1, 1)
            pl.nop().then_inc(S["yall"], 1)

        @block.scalar
        def _(act):
            credit(act, "c_n2", "norm2", "row1", "wfhi", "whi", "smhi", "prob", "pThi", "fhi", "t2hi", "lthi", "tanh", "silu", "hhi", "yThi",
                   "xhi", "esilu", "ehhi")

            for n, factor in enumerate((1.0, SCALE, 1.0)):
                act.wait_ge(S["smT"], done(0))
                act.activation(sm_hi[:, n * C:(n + 1) * C], bank(7, C, n * C), ACT.Copy, scale=factor).then_inc(S["smhi"], 1)
            for n in range(NSH):
                act.wait_ge(S["wT"], done(n))
                act.activation(w_hi[:, n, :], bank(2 * n, WCOLS), ACT.Copy).then_inc(S["whi"], 1)

            def wf_hi(b, j):
                act.wait_ge(S["wfT"], done(4 * b + j))
                alone(act)
                act.activation(w_halves(w_hi, b, j), bank(7, WHALF), ACT.Copy).then_inc(S["wfhi"], 1)

            def fill_hi(b, f):
                act.wait_ge(S["fill"], done(6 * b + f))
                dst = (xT_hi, yT_hi, v_hi)[f // 2]
                if f < 4:
                    act.wait_ge(S["score"], done(TB * b - 1))
                else:
                    act.wait_ge(S["pv"], done(TB * b - 1))
                act.activation(dst[:, f % 2 * 512:f % 2 * 512 + 512], bank((7, 1)[f % 2]), ACT.Copy).then_inc(S["fhi"], 1)

            def exp(b, k):
                i, n = ORDER[k], TB * b + k
                act.wait_ge(S["nmax"], done(n))
                act.wait_ge(S["pT"], done(NCH * b + (CH[k - 1] if k else 0) - 1))
                act.wait_ge(S["x2"], done(TB * b - 1))
                act.activation(prob[k % 2][:, 0:(i + 1) * P], bank(2 * (k % 2), (i + 1) * P), ACT.Exp,
                               bias=nmax[:, i:i + 1], accum_out=rsum[:, i:i + 1]).then_inc(S["prob"], 1)

            def pT_split(b, k, h):
                bk, j0, j1 = chunks(k)[h]
                act.wait_ge(S["pT"], done(NCH * b + CH[k] + h))
                act.wait_ge(S["pv"], done(TB * b + k - 2))
                act.activation(pT_hi[k % 2][:, j0 * P:j1 * P], bank(bk, (j1 - j0) * P), ACT.Copy).then_inc(S["pThi"], 1)

            c_n2 = Chain(act, S["c_n2"], GT)

            def normalise2(i, off):
                g, par = 2 * i + off, off % 2
                c_n2.start(g)
                for t in range(GT):
                    n = bass.ds(g * GT + t, 1)
                    c_n2.inc(act.activation(xn[:, par * GT + t, :], tile_of(x_all, g * GT + t), ACT.Identity,
                                            bias=shift2[:, n], scale=rstd2[:, n]))
                c_n2.end()
                act.nop().then_inc(S["norm2"], 1)

            def t2_hi(i, off, bk=6):
                g = 2 * i + off
                act.wait_ge(S["t2"], done(g))
                act.activation(x2T_hi[off % 2][:], bank(bk), ACT.Copy).then_inc(S["t2hi"], 1)

            def batch_act(b, more):
                for k in range(TB):
                    if k % 2 == 0:
                        exp(b, k)
                    if k >= 1:
                        for h in range(len(chunks(k - 1))):
                            pT_split(b, k - 1, h)
                    if k % 2:
                        exp(b, k)
                    if 1 <= k <= 4:
                        wf_hi(b, k - 1)
                    if not more and k == 5:
                        act.wait_ge(S["shift2"], 1)
                        normalise2(0, 0)
                    if not more and k == 6:
                        normalise2(0, 1)
                if more:
                    fill_hi(b + 1, 0)
                else:
                    t2_hi(0, 0, 7)
                pT_split(b, TB - 1, 0)
                if more:
                    fill_hi(b + 1, 1)
                pT_split(b, TB - 1, 1)
                if more:
                    for f in range(2, 6):
                        fill_hi(b + 1, f)

            for f in range(6):
                fill_hi(0, f)
            with act.Fori(0, B - 1) as b:
                batch_act(b, True)
            batch_act(B - 1, False)

            def rows(i, off):
                g, par = 2 * i + off, off % 2
                act.wait_ge(S["rows_sent"], done(g - 2))
                alone(act)
                for k in range(KTOP):
                    act.activation(xrow[k][par][:, :, 0:C], xn[:, par * GT:(par + 1) * GT, :], ACT.Copy).then_inc(S["row1"], 1)

            def lt_bias(i, off):
                g = 2 * i + off
                act.wait_ge(S["lt"], done(g))
                act.wait_ge(S["r3"], done(g - 1))
                act.activation(logitT[:], bank(6)[0:E, :], ACT.Identity, bias=bias_col[:]).then_inc(S["lthi"], 1)

            def unit_silu(g, u):
                n = 4 * g + u
                act.wait_ge(S["gu"], done(n))
                act.wait_ge(S["mul"], done(n - 2))
                act.activation(sil[u % 2][:], bank(2 * (u % 2)), ACT.Silu).then_inc(S["silu"], 1)

            def unit_hi(g, u):
                n = 4 * g + u
                act.wait_ge(S["mul"], done(n))
                act.wait_ge(S["yT"], done(n - 2))
                act.activation(hT_hi[u % 2][:], hid[u % 2][:], ACT.Copy).then_inc(S["hhi"], 1)

            def weights(g):
                act.wait_ge(S["rt1"], done(g))
                act.activation(gapt[:], gap[:], ACT.Tanh, scale=0.5).then_inc(S["tanh"], 1)

            def shared_copy(i, off):
                g = 2 * i + off
                act.wait_ge(S["yT"], done(4 * g + 3))
                act.wait_ge(S["back"], done(g - 1))
                act.activation(shT[:], bank(4), ACT.Copy).then_inc(S["yThi"], 1)

            def shared_act(i, off, route, norm):
                g = 2 * i + off
                unit_silu(g, 2)
                unit_hi(g, 2)
                if route:
                    t2_hi(i, off + 1)
                unit_silu(g, 3)
                unit_hi(g, 3)
                if route:
                    lt_bias(i, off + 1)
                    unit_silu(g + 1, 0)
                    rows(i, off + 1)
                    unit_hi(g + 1, 0)
                    weights(g + 1)
                shared_copy(i, off)
                if route:
                    unit_silu(g + 1, 1)
                if norm:
                    normalise2(i, off + 2)
                if route:
                    unit_hi(g + 1, 1)

            lt_bias(0, 0)
            rows(0, 0)
            unit_silu(0, 0)
            unit_hi(0, 0)
            weights(0)
            unit_silu(0, 1)
            unit_hi(0, 1)
            act.wait_ge(S["shift2"], 2)
            with act.Fori(0, NG // 2 - 1) as i:
                shared_act(i, 0, True, True)
                shared_act(i, 1, True, True)
            shared_act(NG // 2 - 1, 0, True, False)
            shared_act(NG // 2 - 1, 1, False, False)

            def x_hi(i, off):
                p, par = 2 * i + off, off % 2
                act.wait_ge(S["tx"], done(p))
                act.wait_ge(S["eh"], done(p - 2))
                act.activation(gT_hi[par][:], bank(4, 2 * P), ACT.Copy).then_inc(S["xhi"], 1)

            def e_silu(i, off):
                p, par = 2 * i + off, off % 2
                act.wait_ge(S["eh"], done(p))
                act.wait_ge(S["emul"], done(p - 2))
                act.activation(sil[par][:].rearrange("p (s h) -> p s h", s=2),
                               halves(ps[:, 1024 * par:1024 * par + 1024], 0),
                               ACT.Silu).then_inc(S["esilu"], 1)

            def h_hi(i, off):
                p, par = 2 * i + off, off % 2
                act.wait_ge(S["eth"], done(p))
                act.wait_ge(S["ey"], done(p - 2))
                act.activation(hT_hi[par][:], bank(5), ACT.Copy).then_inc(S["ehhi"], 1)

            def e_step(i, off, x=True, h=True):
                if x:
                    x_hi(i, off + 2)
                if h:
                    e_silu(i, off + 1)
                h_hi(i, off)

            x_hi(0, 0)
            x_hi(0, 1)
            e_silu(0, 0)
            e_step(0, 0)
            with act.Fori(0, PAIRS // 2 - 2) as i:
                e_step(i, 1)
                e_step(i, 2)
            L = PAIRS // 2 - 1
            e_step(L - 1, 1)
            e_step(L, 0, x=False)
            e_step(L, 1, x=False, h=False)

            for n in range(NC):
                act.wait_ge(S["fin"], done(n))
                t = slice(n * CT, (n + 1) * CT)
                act.dma_start(out_rows[:, t, :], x_all[:, t, :]).then_inc(s_out[n % 2], 16)

        @block.vector
        def _(ve):
            credit(ve, "norm1", "c_st1", "rinv", "c_st2", "c_rt1", "c_rt2", "c_tab", "c_cnt", "c_fin", "wflo", "wlo", "smlo", "st1", "nmax", "pTlo", "x2", "flo", "st2", "t2lo", "rt1", "rt2",
                   "mul", "hlo", "addb", "xlo", "emeta", "emul", "ehlo", "eyout", "fin")

            c1 = Chain(ve, S["c_st1"], 2 * TB)

            def stats1(b, first, last):
                if first == 0:
                    c1.start(b)
                for t in range(first, last):
                    c1.inc(ve.bn_stats(stats[:, t, :], tile_of(x_all, b * TB + t)))

            def aggr1(b):
                c1.wait()
                alone(ve)
                for t in range(TB):
                    c1.inc(ve.bn_aggr(mv[:, t, :], stats[:, t, :]))
                c1.end()
                ve.tensor_scalar(veps[:], mv[:, :, 1], EPS, None, ALU.add).then_inc(S["st1"], 1)

            def normalise(b, first, last):
                if first == 0:
                    ve.wait_ge(S["pow1"], done(b))
                    ve.wait_ge(S["fill"], done(6 * b - 2))
                for t in range(first, last):
                    ve.tensor_scalar(xn[:, t, :], tile_of(x_all, b * TB + t), mv[:, t, 0:1], rstd[:, t:t + 1],
                                     ALU.subtract, ALU.mult).then_inc(S["norm1"], 1)

            ve.wait_ge(s_x0, 16)
            stats1(0, 0, TB)
            aggr1(0)
            normalise(0, 0, TB)

            ve.wait_ge(S["smhi"], done(2))
            for n, factor in enumerate((1.0, SCALE, 1.0)):
                c = slice(n * C, (n + 1) * C)
                ve.scalar_tensor_tensor(out=sm_lo[:, c], in0=bank(7, C, n * C), scalar=factor, in1=sm_hi[:, c].bitcast(F32),
                                        op0=ALU.mult, op1=ALU.subtract).then_inc(S["smlo"], 1)

            for n in range(NSH):
                ve.wait_ge(S["whi"], done(n))
                ve.tensor_tensor(w_lo[:, n, :], bank(2 * n, WCOLS), w_hi[:, n, :].bitcast(F32), ALU.subtract).then_inc(S["wlo"], 1)

            def wf_lo(b, j):
                ve.wait_ge(S["wfhi"], done(4 * b + j))
                ve.tensor_tensor(w_halves(w_lo, b, j), bank(7, WHALF), w_halves(w_hi, b, j).bitcast(F32),
                                 ALU.subtract).then_inc(S["wflo"], 1)

            def fill_lo(b, f):
                src_hi = (xT_hi, yT_hi, v_hi)[f // 2]
                dst = (xT_lo, yT_lo, v_lo)[f // 2]
                ve.wait_ge(S["fhi"], done(6 * b + f))
                c = slice(f % 2 * 512, f % 2 * 512 + 512)
                ve.tensor_tensor(dst[:, c], bank((7, 1)[f % 2]), src_hi[:, c].bitcast(F32), ALU.subtract).then_inc(S["flo"], 1)

            def invert(b, k):
                i = ORDER[k]
                ve.reciprocal(rinv[:, i:i + 1], rsum[:, i:i + 1]).then_inc(S["rinv"], 1)

            def row_max(b, k):
                i, n = ORDER[k], TB * b + k
                ve.wait_ge(S["score"], done(n))
                ve.wait_ge(S["prob"], done(TB * b - 1))
                ve.tensor_reduce(nmax[:, i:i + 1], bank(2 * (k % 2), (i + 1) * P), AXX, ALU.max,
                                 negate=True).then_inc(S["nmax"], 1)

            def pT_rest(b, k, h):
                bk, j0, j1 = chunks(k)[h]
                ve.wait_ge(S["pThi"], done(NCH * b + CH[k] + h))
                ve.tensor_tensor(pT_lo[k % 2][:, j0 * P:j1 * P], bank(bk, (j1 - j0) * P),
                                 pT_hi[k % 2][:, j0 * P:j1 * P].bitcast(F32), ALU.subtract).then_inc(S["pTlo"], 1)

            def add_attn(b, k):
                i, n = ORDER[k], TB * b + k
                ve.wait_ge(S["pv"], done(n))
                ve.wait_ge(S["rinv"], done(n))
                xt = tile_of(x_all, TB * b + i)
                ve.scalar_tensor_tensor(out=xt, in0=bank(6, P), scalar=rinv[:, i:i + 1], in1=xt,
                                        op0=ALU.mult, op1=ALU.add).then_inc(S["x2"], 1)

            c_x2 = Chain(ve, S["c_st2"], 2 * TB)

            def stats_2(b, k):
                ve.wait_ge(S["x2"], done(TB * b + k))
                alone(ve)
                c_x2.inc(ve.bn_stats(stats2[:, ORDER[k], :], tile_of(x_all, TB * b + ORDER[k])))

            def aggr_2(b):
                c_x2.wait()
                ve.wait_ge(S["c_st2"], c_x2.base + TB)
                alone(ve)
                for t in range(TB):
                    c_x2.inc(ve.bn_aggr(mv2[:, t, :], stats2[:, t, :]))
                c_x2.end()
                bt = bass.ds(TB * b, TB)
                ve.tensor_copy(mean2[:, bt], mv2[:, :, 0])
                ve.tensor_scalar(veps2[:, bt], mv2[:, :, 1], EPS, None, ALU.add).then_inc(S["st2"], 1)

            def shift_2(first, last):
                ve.wait_ge(S["pow2"], done(last // TB - 1))
                t = slice(first, last)
                ve.scalar_tensor_tensor(out=shift2[:, t], in0=mean2[:, t], scalar=-1.0, in1=rstd2[:, t], op0=ALU.mult,
                                        op1=ALU.mult).then_inc(S["shift2"], 1)

            def t2_lo(i, off, bk=6):
                g = 2 * i + off
                ve.wait_ge(S["t2hi"], done(g))
                ve.tensor_tensor(x2T_lo[off % 2][:], bank(bk), x2T_hi[off % 2][:].bitcast(F32),
                                 ALU.subtract).then_inc(S["t2lo"], 1)

            def batch_dve(b, more):
                c_x2.start(b)
                for k in range(TB):
                    row_max(b, k)
                    if k >= 1:
                        for h in range(len(chunks(k - 1))):
                            pT_rest(b, k - 1, h)
                        invert(b, k - 1)
                    if 1 <= k <= 4:
                        wf_lo(b, k - 1)
                    if k >= 2:
                        add_attn(b, k - 2)
                    if k >= 3:
                        stats_2(b, k - 3)
                    if more and k <= 2:
                        stats1(b + 1, 3 * k, min(3 * k + 3, TB))
                    if more and k == 3:
                        aggr1(b + 1)
                    if more and 4 <= k <= 6:
                        normalise(b + 1, 3 * (k - 4), min(3 * (k - 4) + 3, TB))
                    if not more and k == 3:
                        shift_2(0, (B - 1) * TB)
                if more:
                    fill_lo(b + 1, 0)
                else:
                    t2_lo(0, 0, 7)
                pT_rest(b, TB - 1, 0)
                if more:
                    fill_lo(b + 1, 1)
                pT_rest(b, TB - 1, 1)
                invert(b, TB - 1)
                add_attn(b, TB - 2)
                stats_2(b, TB - 3)
                if more:
                    fill_lo(b + 1, 2)
                    fill_lo(b + 1, 3)
                add_attn(b, TB - 1)
                stats_2(b, TB - 2)
                if more:
                    fill_lo(b + 1, 4)
                    fill_lo(b + 1, 5)
                stats_2(b, TB - 1)
                aggr_2(b)

            for f in range(6):
                fill_lo(0, f)
            ve.wait_ge(s_x1, 16)
            with ve.Fori(0, B - 1) as b:
                batch_dve(b, True)
            batch_dve(B - 1, False)

            c_rt1 = Chain(ve, S["c_rt1"], 2 * GT + 3)
            c_rt2 = Chain(ve, S["c_rt2"], 8)

            def route1(i, off):
                g = 2 * i + off
                c_rt1.start(g)
                ve.wait_ge(S["r3"], done(g))
                alone(ve)
                for t in range(GT):
                    c_rt1.inc(ve.max(top[:, t, :], bank(7, E, t * E)))
                c_rt1.wait()
                alone(ve)
                for t in range(GT):
                    c_rt1.inc(ve.max_index(topi[:, t, :], top[:, t, :], bank(7, E, t * E)))
                c_rt1.wait()
                c_rt1.link(ve.tensor_copy(topf[:], topi[:, :, 0:KTOP].rearrange("p t k -> p k t")))
                c_rt1.inc(ve.tensor_tensor(hot[:], iota_e[:].unsqueeze(1).unsqueeze(1).broadcast_to([P, KTOP, GT, E]),
                                           topf[:].unsqueeze(3).broadcast_to([P, KTOP, GT, E]), ALU.is_equal))
                c_rt1.inc(ve.tensor_tensor(gap[:], top[:, :, 0], top[:, :, 1], ALU.subtract))
                c_rt1.end()
                ve.tensor_tensor(hot_b[:], hot[:, 0], hot[:, 1], ALU.add).then_inc(S["rt1"], 1)

            def route2(i, off):
                g, par = 2 * i + off, off % 2
                c_rt2.start(g)
                ve.wait_ge(S["rk"], done(g))
                ve.wait_ge(S["tanh"], done(g))
                ve.wait_ge(S["rows_sent"], done(g - 2))
                c_rt2.inc(ve.tensor_tensor(place[:], bank(7, GT * E, 64).rearrange("p (t e) -> p t e", e=E),
                                           count[:].unsqueeze(1).broadcast_to([P, GT, E]), ALU.add))
                c_rt2.link(ve.tensor_reduce(added[:], bank(7, GT * E, 128).rearrange("p (t e) -> p e t", e=E), AXX, ALU.add))
                c_rt2.inc(ve.tensor_tensor(count[:], count[:], added[:], ALU.add))
                c_rt2.link(ve.tensor_tensor(picked[:], place[:].unsqueeze(1).broadcast_to([P, KTOP, GT, E]), hot[:], ALU.mult))
                c_rt2.link(ve.tensor_reduce(posf[:], picked[:], AXX, ALU.add))
                c_rt2.inc(ve.tensor_copy(pos[par][:], posf[:]))
                for k in range(KTOP):
                    c_rt2.inc(ve.tensor_scalar(xrow[k][par][:, :, C + 1], gapt[:], 0.5 - k, 0.5, ALU.mult, ALU.add))
                c_rt2.end()
                ve.nop().then_inc(S["rt2"], 1)

            def unit_mul(g, u):
                n = 4 * g + u
                ve.wait_ge(S["silu"], done(n))
                ve.wait_ge(S["hhi"], done(n - 2))
                ve.tensor_tensor(hid[u % 2][:], sil[u % 2][:], bank(2 * (u % 2) + 1), ALU.mult).then_inc(S["mul"], 1)

            def unit_lo(g, u):
                ve.wait_ge(S["hhi"], done(4 * g + u))
                ve.tensor_tensor(hT_lo[u % 2][:], hid[u % 2][:], hT_hi[u % 2][:].bitcast(F32),
                                 ALU.subtract).then_inc(S["hlo"], 1)

            def slot_tables():
                c = Chain(ve, S["c_tab"], 20)
                c.start(0)
                rows, tiles, ends = t8[0], t8[1], t8[2]
                c.inc(ve.tensor_copy(padpos[:], count[0:1, :]))
                c.link(ve.tensor_tensor(rows[:], count[0:1, :], region0[0:1, :], ALU.subtract))
                c.link(ve.tensor_scalar(t8i[:], rows[:], float(P - 1), None, ALU.add))
                c.link(ve.tensor_scalar(t8i[:], t8i[:], 7, None, ALU.arith_shift_right))
                c.link(ve.tensor_copy(tiles[:], t8i[:]))
                c.link(ve.tensor_tensor(t64[:], lower[:], tiles[:].unsqueeze(1).broadcast_to([1, E, E]), ALU.mult))
                c.link(ve.tensor_reduce(ends[:], t64[:], AXX, ALU.add))
                c.link(ve.tensor_tensor(past[:], iota_s[:].unsqueeze(2).broadcast_to([1, SLOTS, E]),
                                        ends[:].unsqueeze(1).broadcast_to([1, SLOTS, E]), ALU.is_ge))
                c.inc(ve.tensor_reduce(slot_e[:], past[:], AXX, ALU.add))
                c.link(ve.tensor_tensor(past2[:], past[:], tiles[:].unsqueeze(1).broadcast_to([1, SLOTS, E]), ALU.mult))
                c.link(ve.tensor_reduce(slot_t[:], past2[:], AXX, ALU.add))
                c.link(ve.tensor_scalar(slot_w[:], slot_e[:], float(E - 1), float(NSH), ALU.min, ALU.add))
                w2v = slot_w[:].rearrange("o (p k) -> o p k", k=2)
                c.link(ve.scalar_tensor_tensor(out=pair_w[:], in0=w2v[:, :, 1], scalar=16.0, in1=w2v[:, :, 0],
                                               op0=ALU.mult, op1=ALU.add))
                c.link(ve.memset(step_w[:], 0.0))
                c.link(ve.tensor_copy(step_w[:, 0:PAIRS], pair_w[:]))
                c.link(ve.scalar_tensor_tensor(out=step_w[:, 3:PAIRS + 3], in0=pair_w[:], scalar=256.0,
                                               in1=step_w[:, 3:PAIRS + 3], op0=ALU.mult, op1=ALU.add))
                c.inc(ve.tensor_copy(step_wi[:], step_w[:]))
                c.link(ve.tensor_tensor(slot_w[:], iota_s[:], slot_t[:], ALU.subtract))
                c.link(ve.tensor_scalar(slot_r[:], slot_w[:], float(P), None, ALU.mult))
                c.link(ve.scalar_tensor_tensor(out=slot_ri[:], in0=slot_e[:], scalar=float(REGION), in1=slot_r[:],
                                               op0=ALU.mult, op1=ALU.add))
                c.end()
                ve.nop().then_inc(S["tab"], 1)

            def add_shared(i, off):
                g = 2 * i + off
                ve.wait_ge(S["back"], done(g))
                xg4 = x_all[:, bass.ds(g * GT, GT), :]
                ve.tensor_tensor(xg4, xg4, bank(5).rearrange("p (t c) -> p t c", c=C), ALU.add).then_inc(S["addb"], 1)

            def shared_dve(i, off, route):
                g = 2 * i + off
                unit_mul(g, 2)
                unit_lo(g, 2)
                if route:
                    t2_lo(i, off + 1)
                unit_mul(g, 3)
                unit_lo(g, 3)
                if route:
                    route1(i, off + 1)
                    unit_mul(g + 1, 0)
                    unit_lo(g + 1, 0)
                    route2(i, off + 1)
                    unit_mul(g + 1, 1)
                    unit_lo(g + 1, 1)
                else:
                    slot_tables()
                add_shared(i, off)

            ve.wait_ge(S["const"], 1)
            c_cnt = Chain(ve, S["c_cnt"], 1)
            c_cnt.start(0)
            c_cnt.link(ve.tensor_copy(count[:], region0[:]))
            shift_2((B - 1) * TB, NT)
            unit_mul(0, 0)
            unit_lo(0, 0)
            route1(0, 0)
            unit_mul(0, 1)
            unit_lo(0, 1)
            route2(0, 0)
            with ve.Fori(0, NG // 2 - 1) as i:
                shared_dve(i, 0, True)
                shared_dve(i, 1, True)
            shared_dve(NG // 2 - 1, 0, True)
            shared_dve(NG // 2 - 1, 1, False)

            def x_lo(i, off):
                p, par = 2 * i + off, off % 2
                for k in range(2):
                    ve.wait_ge(s_xg[2 * par + k], (i + off // 2 + 1) * 16)
                ve.tensor_copy(meta[:, bass.ds(2 * p, 2), :], xg[:, 2 * par:2 * par + 2, C:C + 2]).then_inc(S["emeta"], 1)
                ve.wait_ge(S["xhi"], done(p))
                ve.tensor_tensor(gT_lo[par][:], bank(4, 2 * P), gT_hi[par][:].bitcast(F32), ALU.subtract).then_inc(S["xlo"], 1)

            def e_mul(i, off):
                p, par = 2 * i + off, off % 2
                ve.wait_ge(S["esilu"], done(p))
                ve.wait_ge(S["eth"], done(p - 2))
                ve.tensor_tensor(hid[par][:].rearrange("p (s h) -> p s h", s=2), sil[par][:].rearrange("p (s h) -> p s h", s=2),
                                 halves(ps[:, 1024 * par:1024 * par + 1024], 1), ALU.mult).then_inc(S["emul"], 1)

            def h_lo(i, off):
                p, par = 2 * i + off, off % 2
                ve.wait_ge(S["ehhi"], done(p))
                ve.tensor_tensor(hT_lo[par][:], bank(5), hT_hi[par][:].bitcast(F32), ALU.subtract).then_inc(S["ehlo"], 1)

            def y_out(i, off):
                p, par = 2 * i + off, off % 2
                ve.wait_ge(S["ey"], done(p))
                ve.wait_ge(S["ysent"], done(p - 2))
                ve.wait_ge(S["emeta"], done(p))
                for k in range(2):
                    ve.tensor_scalar(yrow[2 * par + k][:], bank(6, P, k * P),
                                     meta[:, bass.ds(2 * p + k, 1), 1], None, ALU.mult).then_inc(S["eyout"], 1)

            def e_step(i, off, x=True, h=True, y=True):
                if x:
                    x_lo(i, off + 2)
                if h:
                    e_mul(i, off + 1)
                h_lo(i, off)
                if y:
                    y_out(i, off - 1)

            x_lo(0, 0)
            x_lo(0, 1)
            e_mul(0, 0)
            e_step(0, 0, y=False)
            with ve.Fori(0, PAIRS // 2 - 2) as i:
                e_step(i, 1)
                e_step(i, 2)
            L = PAIRS // 2 - 1
            e_step(L - 1, 1)
            e_step(L, 0, x=False)
            e_step(L, 1, x=False, h=False)
            y_out(L, 1)

            c_fin = Chain(ve, S["c_fin"], NC)
            c_fin.start(0)
            for n in range(NC):
                ve.wait_ge(s_yb[n], 2 * 16)
                xc = x_all[:, n * CT:(n + 1) * CT, :]
                c_fin.link(ve.tensor_tensor(xc, xc, yb[0][n % RING], ALU.add))
                ve.tensor_tensor(xc, xc, yb[1][n % RING], ALU.add).then_inc(S["fin"], 1)

        @block.tensor
        def _(pe):
            credit(pe, "wfT", "wT", "smT", "score", "pT", "pv", "fill", "t2", "lt", "r3", "rk", "gu", "yT", "back",
                   "tx", "eh", "eth", "ey")

            def product(dst, a_hi, a_lo, b_hi, b_lo, start=True, stop=True):
                pe.matmul(dst, a_lo, b_hi, start=start, stop=False)
                pe.matmul(dst, a_hi, b_lo, start=False, stop=False)
                return pe.matmul(dst, a_hi, b_hi, start=False, stop=stop)

            pe.wait_ge(S["const"], 1)
            pe.wait_ge(s_small, 5 * 16)
            pe.transpose(bank(7, P), wqkv[:, 2, :], ident[:])
            pe.matmul(bank(7, P, P), wqkv[:, 0, :], wqkv[:, 1, :], start=True, stop=True)
            pe.transpose(bank(7, P, 2 * P), rw_raw[:], ident[:]).then_inc(S["smT"], 1)
            wv_hi, wv_lo = sm_hi[:, 0:C], sm_lo[:, 0:C]
            m_hi, m_lo = sm_hi[:, C:2 * C], sm_lo[:, C:2 * C]
            r_hi, r_lo = sm_hi[:, 2 * C:SM], sm_lo[:, 2 * C:SM]

            for n in range(NSH):
                pe.wait_ge(s_raw[n], 3 * 16)
                for j in range(WBLK):
                    last = pe.transpose(bank(2 * n, P, j * P), raw[n][:, j, :], ident[:])
                last.then_inc(S["wT"], 1)

            def wf_transpose(b, j):
                pe.wait_ge(s_raw[j // 2], (b + 2) * 3 * 16)
                pe.wait_ge(S["wflo"], done(4 * b + j - 1))
                for m in range(3):
                    last = pe.transpose(bank(7, P, m * P), raw[j // 2][:, j % 2 * 3 + m, :], ident[:])
                last.then_inc(S["wfT"], 1)
                if j % 2:
                    pe.wait_ge(S["wfT"], done(4 * b + j))
                    pe.sem_inc(S["wT"], 1)

            def fill(b, f):
                dst = bank((7, 1)[f % 2])
                pe.wait_ge(S["flo"], done(6 * b + f - 2))
                if f < 2:
                    if f == 0:
                        pe.wait_ge(S["norm1"], done(TB * b + TB - 1))
                    for j in range(4):
                        last = pe.transpose(dst[:, j * P:(j + 1) * P], xn[:, 4 * f + j, :], ident[:])
                elif f < 4:
                    c = slice(f % 2 * 512, f % 2 * 512 + 512)
                    last = product(dst, m_hi, m_lo, xT_hi[:, c], xT_lo[:, c])
                else:
                    for j in range(4):
                        c = slice((f % 2 * 4 + j) * P, (f % 2 * 4 + j + 1) * P)
                        last = product(dst[:, j * P:(j + 1) * P], xT_hi[:, c], xT_lo[:, c], wv_hi, wv_lo)
                last.then_inc(S["fill"], 1)

            def score(b, k):
                i, n = ORDER[k], TB * b + k
                pe.wait_ge(S["prob"], done(n - 2))
                q = slice(i * P, (i + 1) * P)
                width = (i + 1) * P
                base = 2 * (k % 2)
                for c0 in range(0, width, 512):
                    c1 = min(c0 + 512, width)
                    product(bank(base, c1 - c0, c0), yT_hi[:, q], yT_lo[:, q], xT_hi[:, c0:c1], xT_lo[:, c0:c1],
                            stop=c1 < width)
                pe.matmul(bank(base, P, i * P), ident_b[:], mask_b[:], start=False, stop=True).then_inc(S["score"], 1)

            def p_transpose(b, k, h):
                bk, j0, j1 = chunks(k)[h]
                if h == 0:
                    pe.wait_ge(S["prob"], done(TB * b + k))
                pe.wait_ge(S["pTlo"], done(NCH * b + CH[k] + h - 3))
                for j in range(j0, j1):
                    last = pe.transpose(bank(bk, P, (j - j0) * P), prob[k % 2][:, j * P:(j + 1) * P], ident[:])
                last.then_inc(S["pT"], 1)

            def pv(b, k, h):
                bk, j0, j1 = chunks(k)[h]
                i = ORDER[k]
                pe.wait_ge(S["pTlo"], done(NCH * b + CH[k] + h))
                if h == 0:
                    pe.wait_ge(S["x2"], done(TB * b + k - 1))
                for j in range(j0, j1):
                    c = slice(j * P, (j + 1) * P)
                    last = product(bank(6, P), pT_hi[k % 2][:, c], pT_lo[k % 2][:, c], v_hi[:, c], v_lo[:, c],
                                   start=j == 0, stop=j == i)
                if j1 == i + 1:
                    last.then_inc(S["pv"], 1)

            def t2(i, off, bk=6):
                g, par = 2 * i + off, off % 2
                pe.wait_ge(S["norm2"], done(g))
                pe.wait_ge(S["lthi"], done(g - 1))
                for t in range(GT):
                    last = pe.transpose(bank(bk, P, t * P), xn[:, par * GT + t, :], ident[:])
                last.then_inc(S["t2"], 1)

            def batch_pe(b, more):
                for k in range(TB):
                    score(b, k)
                    if k == 1:
                        pe.wait_ge(S["flo"], done(6 * b + 5))
                    if k == TB - 1:
                        pe.wait_ge(S["wflo"], done(4 * b + 3))
                        if more:
                            fill(b + 1, 0)
                        else:
                            t2(0, 0, 7)
                    if k >= 1:
                        for h in range(len(chunks(k - 1))):
                            p_transpose(b, k - 1, h)
                    if 1 <= k <= 4:
                        wf_transpose(b, k - 1)
                    if k >= 2:
                        for h in range(len(chunks(k - 2))):
                            pv(b, k - 2, h)
                p_transpose(b, TB - 1, 0)
                if more:
                    pe.wait_ge(S["pTlo"], done(NCH * b + CH[TB - 2]))
                    fill(b + 1, 1)
                p_transpose(b, TB - 1, 1)
                pv(b, TB - 2, 0)
                if more:
                    fill(b + 1, 2)
                pv(b, TB - 1, 0)
                if more:
                    fill(b + 1, 3)
                pv(b, TB - 1, 1)
                if more:
                    fill(b + 1, 4)
                    fill(b + 1, 5)

            pe.wait_ge(S["smlo"], done(2))
            pe.wait_ge(S["wlo"], done(NSH - 1))
            for f in range(6):
                fill(0, f)
            with pe.Fori(0, B - 1) as b:
                batch_pe(b, True)
            batch_pe(B - 1, False)

            def logits_T(i, off):
                g = 2 * i + off
                pe.wait_ge(S["t2lo"], done(g))
                product(bank(6), r_hi, r_lo, x2T_hi[off % 2][:], x2T_lo[off % 2][:]).then_inc(S["lt"], 1)

            def logits(i, off):
                g = 2 * i + off
                pe.wait_ge(S["lthi"], done(g))
                pe.wait_ge(S["rt2"], done(g - 1))
                alone(pe)
                for t in range(GT):
                    last = pe.transpose(bank(7, E, t * E), logitT[:, t * P:(t + 1) * P], ident[0:E, 0:E])
                last.then_inc(S["r3"], 1)

            def ranks(i, off):
                g = 2 * i + off
                pe.wait_ge(S["rt1"], done(g))
                pe.wait_ge(S["rt2"], done(g - 1))
                hot2 = hot_b[:].rearrange("p t e -> p (t e)")
                pe.matmul(bank(7, GT * E, 64), upper_b[:], hot2, start=True, stop=False)
                for t in range(GT - 1):
                    pe.matmul(bank(7, (GT - 1 - t) * E, 64 + (t + 1) * E).rearrange("p (t e) -> p t e", e=E), ones_b[:],
                              hot_b[:, t:t + 1, :].broadcast_to([P, GT - 1 - t, E]), start=False, stop=t == GT - 2)
                pe.matmul(bank(7, GT * E, 128), ones_b[:], hot2, start=True, stop=True).then_inc(S["rk"], 1)

            def unit_up(i, off, u):
                g = 2 * i + off
                pe.wait_ge(S["mul"], done(4 * g + u - 2))
                xs, j = u // 2, u % 2
                for n in range(2):
                    c = slice((2 * n + j) * P, (2 * n + j + 1) * P)
                    last = product(bank(2 * (u % 2) + n), w_hi[:, xs, c], w_lo[:, xs, c], x2T_hi[off % 2][:], x2T_lo[off % 2][:])
                last.then_inc(S["gu"], 1)

            def unit_down(i, off, u):
                g = 2 * i + off
                xs, j = u // 2, u % 2
                c = slice((4 + j) * P, (5 + j) * P)
                pe.wait_ge(S["hlo"], done(4 * g + u))
                if u == 0:
                    pe.wait_ge(S["yThi"], done(g - 1))
                product(bank(4), w_hi[:, xs, c], w_lo[:, xs, c], hT_hi[u % 2][:], hT_lo[u % 2][:],
                        start=u == 0, stop=u == 3).then_inc(S["yT"], 1)

            def shared_back(i, off):
                g = 2 * i + off
                pe.wait_ge(S["yThi"], done(g))
                pe.wait_ge(S["addb"], done(g - 1))
                for t in range(GT):
                    last = pe.transpose(bank(5, P, t * P), shT[:, t * P:(t + 1) * P], ident[:])
                last.then_inc(S["back"], 1)

            def shared_pe(i, off, route):
                unit_up(i, off, 2)
                unit_down(i, off, 0)
                if route:
                    t2(i, off + 1)
                unit_up(i, off, 3)
                unit_down(i, off, 1)
                if route:
                    logits_T(i, off + 1)
                    unit_up(i, off + 1, 0)
                    logits(i, off + 1)
                unit_down(i, off, 2)
                unit_down(i, off, 3)
                if route:
                    unit_up(i, off + 1, 1)
                    ranks(i, off + 1)
                shared_back(i, off)

            pe.wait_ge(S["x2"], done(NT - 1))
            logits_T(0, 0)
            unit_up(0, 0, 0)
            logits(0, 0)
            unit_up(0, 0, 1)
            ranks(0, 0)
            with pe.Fori(0, NG // 2 - 1) as i:
                shared_pe(i, 0, True)
                shared_pe(i, 1, True)
            shared_pe(NG // 2 - 1, 0, True)
            shared_pe(NG // 2 - 1, 1, False)

            def step_experts(n):
                v = pe.value_load(step_wi[0:1, n])
                return [[bass.ds(nc.s_assert_within(pe.snap((v >> (8 * m + 4 * k)) & 15), NSH, NX - 1,
                                                    skip_runtime_bounds_check_because="slot_tables keeps them in range"), 1)
                         for k in range(2)] for m in range(2)]

            def x_transpose(i, off):
                p, par = 2 * i + off, off % 2
                for k in range(2):
                    pe.wait_ge(s_xg[2 * par + k], (i + off // 2 + 1) * 16)
                pe.wait_ge(S["xlo"], done(p - 1))
                for k in range(2):
                    last = pe.transpose(bank(4, P, k * P), xg[:, 2 * par + k, 0:C], ident[:])
                last.then_inc(S["tx"], 1)

            def up(i, off, which):
                p, par = 2 * i + off, off % 2
                pe.wait_ge(S["xlo"], done(p))
                pe.wait_ge(S["emul"], done(p - 2))
                for k in range(2):
                    e = which[k]
                    c = slice(k * P, (k + 1) * P)
                    last = product(bank(2 * par + k), gT_hi[par][:, c], gT_lo[par][:, c],
                                   w_hi[:, e, 0:2 * HID].rearrange("p o c -> p (o c)"),
                                   w_lo[:, e, 0:2 * HID].rearrange("p o c -> p (o c)"))
                last.then_inc(S["eh"], 1)

            def h_transpose(i, off):
                p, par = 2 * i + off, off % 2
                pe.wait_ge(S["emul"], done(p))
                pe.wait_ge(S["ehlo"], done(p - 1))
                for j in range(4):
                    last = pe.transpose(bank(5, P, j * P), hid[par][:, j * P:(j + 1) * P], ident[:])
                last.then_inc(S["eth"], 1)

            def down(i, off, which):
                p, par = 2 * i + off, off % 2
                pe.wait_ge(S["ehlo"], done(p))
                pe.wait_ge(S["eyout"], done(2 * p - 1))
                for k in range(2):
                    e = which[k]
                    for j in range(2):
                        c = slice((2 * k + j) * P, (2 * k + j + 1) * P)
                        o = 2 * HID + j * C
                        last = product(bank(6, P, k * P), hT_hi[par][:, c], hT_lo[par][:, c],
                                       w_hi[:, e, o:o + C].rearrange("p o c -> p (o c)"),
                                       w_lo[:, e, o:o + C].rearrange("p o c -> p (o c)"), start=j == 0, stop=j == 1)
                last.then_inc(S["ey"], 1)

            def e_step(i, off, x=True, h=True, y=True):
                for_up, for_down = step_experts(bass.ds(2 * i + off + 2, 1))
                h_transpose(i, off)
                if y:
                    down(i, off - 1, for_down)
                if x:
                    x_transpose(i, off + 3)
                if h:
                    up(i, off + 2, for_up)

            pe.wait_ge(S["tab"], 1)
            pe.wait_ge(S["addb"], done(NG - 1))
            x_transpose(0, 0)
            x_transpose(0, 1)
            up(0, 0, step_experts(slice(0, 1))[0])
            x_transpose(0, 2)
            up(0, 1, step_experts(slice(1, 2))[0])
            e_step(0, 0, y=False)
            L = PAIRS // 2 - 1
            with pe.Fori(0, L - 1) as i:
                e_step(i, 1)
                e_step(i, 2)
            e_step(L - 1, 1, x=False)
            e_step(L, 0, x=False, h=False)
            e_step(L, 1, x=False, h=False)
            down(L, 1, step_experts(slice(PAIRS + 2, PAIRS + 3))[1])


INPUTS = ["L0_attn_x", "L0_attn_Wk", "L0_attn_Wq", "L0_attn_Wv", "L0_ffn_router_w", "L0_ffn_expert_bias",
          "L0_ffn_w1", "L0_ffn_w3", "L0_ffn_w2", "L0_ffn_sw1", "L0_ffn_sw3", "L0_ffn_sw2"]


def kernel(**inputs):
    import numpy as np
    import concourse.bacc as bacc
    from concourse.bass_utils import run_bass_kernel_spmd

    nc = bacc.Bacc("TRN2", target_bir_lowering=False, num_devices=1)
    arrays, args = {}, []
    for name in INPUTS:
        a = np.ascontiguousarray(inputs[name])
        arrays[name] = a
        args.append(nc.dram_tensor(name, a.shape, mybir.dt.from_np(a.dtype), kind="ExternalInput").ap())
    shape = arrays["L0_attn_x"].shape
    tokens, experts = shape[0] * shape[1], arrays["L0_ffn_w1"].shape[0]
    out = nc.dram_tensor("out", shape, F32, kind="ExternalOutput").ap()
    xbuf = nc.dram_tensor("xbuf", (experts * (tokens + P) + 8 * P, shape[2] + 2), F32).ap()
    ybuf = nc.dram_tensor("ybuf", (2 * tokens, shape[2]), F32).ap()
    build(nc, *args, out, xbuf, ybuf)
    r = run_bass_kernel_spmd(nc, [arrays], core_ids=[0])
    return r.results[0]["out"]
```

```python
from contextlib import ExitStack

import concourse.bass as bass
from concourse import mybir

F32 = mybir.dt.float32
F32R = mybir.dt.float32r
BF16 = mybir.dt.bfloat16
I32 = mybir.dt.int32
U32 = mybir.dt.uint32
ALU = mybir.AluOpType
ACT = mybir.ActivationFunctionType
AXX = mybir.AxisListType.X

P = 128
CREDIT = 3
EPS = 1e-5
MASKED = -3.0e38


def done(n):
    return n + 1 + CREDIT


class Chain:

    def __init__(self, eng, sem, per):
        self.eng, self.sem, self.per = eng, sem, per

    def start(self, n):
        self.base, self.k = CREDIT + n * self.per, 0

    def inc(self, ins):
        self.k += 1
        ins.then_inc(self.sem, 1)

    def link(self, ins):
        self.inc(ins)
        self.wait()

    def wait(self):
        self.eng.wait_ge(self.sem, self.base + self.k)

    def end(self):
        self.wait()
        assert self.k == self.per, self.k


def build(nc, x, wk, wq, wv, router_w, expert_bias, w1, w3, w2, sw1, sw3, sw2, out, xbuf, ybuf):
    B, T, C = x.shape
    E, HID, _ = w1.shape
    NSH = sw1.shape[0]
    NX = NSH + E
    NTOK = B * T
    NT = NTOK // P
    TB = T // P
    KTOP = 2
    REGION = NTOK + P
    ROW = C + 2
    SLOTS = 4 * -(-((KTOP * NTOK + E * (P - 1)) // P) // 4)
    PAIRS = SLOTS // 2
    SPARE = SLOTS - KTOP * NTOK // P
    GT = 4
    NG = NT // GT
    WCOLS = 2 * HID + HID // P * C
    WBLK = WCOLS // P
    SCALE = float(C) ** -0.5
    assert C == P and HID == 2 * P and SPARE <= 8 and E == 8 and SLOTS % 4 == 0

    x_rows = x.rearrange("b (t p) c -> p (b t) c", p=P)
    out_rows = out.rearrange("b (t p) c -> p (b t) c", p=P)

    with ExitStack() as ctx:
        def sb(name, shape, dt=F32):
            return ctx.enter_context(nc.sbuf_tensor(name, shape, dt))

        def sem(name):
            return ctx.enter_context(nc.semaphore(name))

        x_all = sb("x_all", [P, NT, C])
        w_parts = sb("w_parts", [P, NX, WBLK, 2, P], F32R)
        raw = [sb(f"raw{n}", [P, WBLK, P]) for n in range(2)]
        wqkv = sb("wqkv", [P, 3, C])
        rw_raw = sb("rw_raw", [P, C])
        bias_col = sb("bias_col", [E, 1])
        SM = 3 * C
        sm_hi = sb("sm_hi", [P, SM], F32R)
        sm_lo = sb("sm_lo", [P, SM], F32R)
        ident = sb("ident", [P, P])
        ident_b = sb("ident_b", [P, P], BF16)
        ones_b = sb("ones_b", [P, P], BF16)
        upper_b = sb("upper_b", [P, P], BF16)
        mask_b = sb("mask_b", [P, P], BF16)
        mhalf = sb("mhalf", [P, TB])
        iota_e = sb("iota_e", [P, E])
        region0 = sb("region0", [P, E])
        padrow = sb("padrow", [P, ROW])
        row_id = sb("row_id", [P, KTOP, NT], I32)

        stats = sb("stats", [P, TB, 6])
        mv = sb("mv", [P, TB, 2])
        veps = sb("veps", [P, TB])
        rstd = sb("rstd", [P, TB])
        shift = sb("shift", [P, TB])
        xn = sb("xn", [P, TB, C])
        xT_hi = sb("xT_hi", [P, T], F32R)
        xT_lo = sb("xT_lo", [P, T], F32R)
        yT_hi = sb("yT_hi", [P, T], F32R)
        yT_lo = sb("yT_lo", [P, T], F32R)
        v_hi = sb("v_hi", [P, T], F32R)
        v_lo = sb("v_lo", [P, T], F32R)
        prob = [sb(f"prob{n}", [P, T]) for n in range(2)]
        pT_hi = [sb(f"pT_hi{n}", [P, T], F32R) for n in range(2)]
        pT_lo = [sb(f"pT_lo{n}", [P, T], F32R) for n in range(2)]
        nmax = sb("nmax", [P, TB])
        rsum = sb("rsum", [P, TB])
        rinv = sb("rinv", [P, TB])

        stats2 = sb("stats2", [P, TB, 6])
        mv2 = sb("mv2", [P, TB, 2])
        veps2_p = sb("veps2_p", [P, TB + NT])
        veps2 = veps2_p[:, TB:]
        mean2_p = sb("mean2_p", [P, TB + NT])
        mean2 = mean2_p[:, TB:]
        rstd2_p = sb("rstd2_p", [P, TB + NT])
        rstd2 = rstd2_p[:, TB:]
        shift2 = sb("shift2", [P, NT])
        xrow = [[sb(f"xrow{k}{n}", [P, GT, ROW]) for n in range(2)] for k in range(KTOP)]
        x2T_hi = [sb(f"x2T_hi{n}", [P, GT * P], F32R) for n in range(2)]
        x2T_lo = [sb(f"x2T_lo{n}", [P, GT * P], F32R) for n in range(2)]
        logitT = sb("logitT", [E, GT * P])
        logit = sb("logit", [P, GT, E])
        top = sb("top", [P, GT, 8])
        topi = sb("topi", [P, GT, 8], U32)
        topf = sb("topf", [P, KTOP, GT])
        hot = sb("hot", [P, KTOP, GT, E])
        hot_b = sb("hot_b", [P, GT, E], BF16)
        gap = sb("gap", [P, GT])
        gapt = sb("gapt", [P, GT])
        count = sb("count", [P, E])
        added = sb("added", [P, E])
        place = sb("place", [P, GT, E])
        picked = sb("picked", [P, KTOP, GT, E])
        posf = sb("posf", [P, KTOP, GT])
        pos = [sb(f"pos{n}", [P, KTOP, GT], I32) for n in range(2)]
        sil = [sb(f"sil{n}", [P, 512]) for n in range(2)]
        hid = [sb(f"hid{n}", [P, 512]) for n in range(2)]
        hT_hi = [sb(f"hT_hi{n}", [P, 512], F32R) for n in range(2)]
        hT_lo = [sb(f"hT_lo{n}", [P, 512], F32R) for n in range(2)]
        shT = sb("shT", [P, GT * P])

        padpos = sb("padpos", [1, E], I32)
        t8 = [sb(f"t8_{n}", [1, E]) for n in range(5)]
        t8i = sb("t8i", [1, E], I32)
        lower = sb("lower", [1, E, E])
        t64 = sb("t64", [1, E, E])
        iota_s = sb("iota_s", [1, SLOTS])
        past = sb("past", [1, SLOTS, E])
        past2 = sb("past2", [1, SLOTS, E])
        slot_e = sb("slot_e", [1, SLOTS])
        slot_t = sb("slot_t", [1, SLOTS])
        slot_w = sb("slot_w", [1, SLOTS])
        step_w = sb("step_w", [1, PAIRS + 4])
        step_wi = sb("step_wi", [1, PAIRS // 2 + 2], I32)
        slot_ri = sb("slot_ri", [1, SLOTS], I32)
        xg = sb("xg", [P, 4, ROW])
        meta = sb("meta", [P, SLOTS, 2])
        gT_hi = [sb(f"gT_hi{n}", [P, 2 * P], F32R) for n in range(2)]
        gT_lo = [sb(f"gT_lo{n}", [P, 2 * P], F32R) for n in range(2)]
        yrow = [sb(f"yrow{n}", [P, C]) for n in range(4)]
        ylo = [sb(f"ylo{n}", [P, C]) for n in range(4)]
        yid = [sb(f"yid{n}", [P, 1], I32) for n in range(4)]
        NC = 8
        CT = NT // NC
        RING = 4
        yb11 = sb("yb11", [P, T])
        parts = [a[:, h * CT * C:(h + 1) * CT * C].rearrange("p (t c) -> p t c", c=C)
                 for a in (prob[0][:], prob[1][:], xn[:].rearrange("p t c -> p (t c)"), yb11[:]) for h in range(2)]
        yb = [parts[0:RING], parts[RING:2 * RING]]
        PARTS = [(n, 0, CT) for n in range(NC - 1)] + [(NC - 1, 0, CT // 2), (NC - 1, CT // 2, CT)]
        PARTS = [(0, 0, CT // 2), (0, CT // 2, CT)] + PARTS[1:]
        NPART = len(PARTS)

        ps = ctx.enter_context(nc.psum_tensor("ps", [P, 8 * 512], F32))

        def bank(n, cols=512, first=0):
            return ps[:, n * 512 + first:n * 512 + first + cols]

        def tile_of(a, t):
            return a[:, bass.ds(t, 1), :].rearrange("p o c -> p (o c)")

        HBLK = WBLK // 2

        def routed_half(b, j, part):
            half = w_parts[:, :, j % 2 * HBLK:(j % 2 + 1) * HBLK, part, :]
            return half[:, bass.ds(NSH + 2 * b + j // 2, 1), :, :].rearrange("p o m c -> p (o m) c")

        def blocks(a):
            return a.rearrange("p (m c) -> p m c", c=P)

        ORDER = [n // 2 if n % 2 == 0 else TB - 1 - n // 2 for n in range(TB)]

        def chunks(k):
            i = ORDER[k]
            if k % 2 == 0:
                return [(1, 0, i + 1)]
            return [(4, 0, 4), (5, 4, i + 1)]

        FILL_BANK = (7, 1, 7, 1, 4, 5)
        CH = [sum(len(chunks(m)) for m in range(k)) for k in range(TB)]
        NCH = CH[-1] + len(chunks(TB - 1))

        def halves(a, k):
            return a.rearrange("p (s h) -> p s h", s=2)[:, :, k * HID:(k + 1) * HID]

        def alone(eng):
            eng.sem_inc(S["passed"], 1)

        s_x0 = sem("s_x0")
        s_x1 = sem("s_x1")
        s_small = sem("s_small")
        s_raw = [sem(f"s_raw{n}") for n in range(2)]
        s_pad0 = sem("s_pad0")
        s_rows = [sem(f"s_rows{n}") for n in range(2)]
        s_padw = sem("s_padw")
        s_xg = [sem(f"s_xg{n}") for n in range(4)]
        s_yw = [sem(f"s_yw{n}") for n in range(4)]
        s_yb = [[sem(f"s_yb{k}{n}") for n in range(NC)] for k in range(KTOP)]
        s_out = [sem(f"s_out{n}") for n in range(2)]
        S = {n: sem("s_" + n) for n in (
            "c_const c_norm2 c_yid c_st1 c_st2 c_agg c_n2 c_cnt c_rt1 c_rt2 c_tab c_tab2 c_fin passed "
            "zeroed const smT smhi smlo wT whi wlo wfT wfhi wflo "
            "st1 pow1 shift1 norm1 fill fhi flo score nmax prob pT pThi pTlo rinv pv x2 "
            "filled2 st2 pow2 shift2 "
            "norm2 row1 t2 t2hi t2lo lt lthi r3 rt1 rk rt2 tanh rows_sent gu silu mul hhi hlo yT yThi back addb "
            "padpos tabr tab tx xhi xlo emeta eh esilu emul eth ehhi ehlo ey ylo eyout ysent yall "
            "fin").split()}

        block = ctx.enter_context(nc.Block())

        def credit(eng, *which):
            for n in which:
                eng.sem_inc(S[n], CREDIT)

        @block.sync
        def _(sp):
            sp.dma_start(x_all[:, 0:TB, :], x_rows[:, 0:TB, :]).then_inc(s_x0, 16)
            for n, w in enumerate((wq, wk, wv)):
                sp.dma_start(wqkv[:, n, :], w).then_inc(s_small, 16)
            sp.wait_ge(S["zeroed"], 1)
            sp.dma_start(rw_raw[0:E, :], router_w).then_inc(s_small, 16)
            sp.dma_start(bias_col[:], expert_bias.rearrange("(e o) -> e o", o=1)).then_inc(s_small, 16)

            def load_expert(par, a1, a3, a2):
                for n, a in enumerate((a1, a3)):
                    sp.dma_start(raw[par][:, 2 * n:2 * n + 2, :],
                                 a.rearrange("o (j p) c -> p (o j) c", p=P)).then_inc(s_raw[par], 16)
                sp.dma_start(raw[par][:, 4:6, :].rearrange("p j c -> p (j c)"),
                             a2.rearrange("o p h -> p (o h)")).then_inc(s_raw[par], 16)

            for n in range(NSH):
                load_expert(n, sw1[n:n + 1], sw3[n:n + 1], sw2[n:n + 1])
            sp.dma_start(x_all[:, TB:NT, :], x_rows[:, TB:NT, :]).then_inc(s_x1, 16)
            with sp.Fori(0, B) as b:
                for k in range(2):
                    sp.wait_ge(S["wT"], done(k))
                    sp.wait_ge(S["wfT"], done(4 * b + 2 * k - 3))
                    e = bass.ds(2 * b + k, 1)
                    load_expert(k, w1[e, :, :], w3[e, :, :], w2[e, :, :])
            sp.wait_ge(S["const"], 1)
            for n in range(8):
                r = E * REGION + n * P
                sp.dma_start(xbuf[r:r + P, :], padrow[:]).then_inc(s_pad0, 16)

            sp.wait_ge(s_pad0, 8 * 16)
            sp.wait_ge(S["padpos"], 1)
            for e in range(E):
                r = sp.value_load(padpos[0:1, e:e + 1], min_val=0, max_val=E * REGION - P)
                sp.dma_start(xbuf[bass.ds(r, P), :], padrow[:]).then_inc(s_padw, 16)
            sp.wait_ge(S["tabr"], 1)
            first = [sp.value_load(slot_ri[0:1, q:q + 1], min_val=0, max_val=E * REGION + 7 * P) for q in range(4)]
            sp.wait_ge(s_padw, E * 16)
            for par in range(2):
                sp.wait_ge(s_rows[par], NG // 2 * GT * KTOP * 16)

            for q in range(4):
                sp.dma_start(xg[:, q, :], xbuf[bass.ds(first[q], P), :]).then_inc(s_xg[q], 16)

            def load_slots(i, off):
                p, par = 2 * i + off, off % 2
                sp.wait_ge(S["tx"], done(p - 2))
                sp.wait_ge(S["emeta"], done(p - 2))
                for k in range(2):
                    r = sp.value_load(slot_ri[0:1, bass.ds(2 * p + k, 1)], min_val=0, max_val=E * REGION + 7 * P)
                    q = 2 * par + k
                    sp.dma_start(xg[:, q, :], xbuf[bass.ds(r, P), :]).then_inc(s_xg[q], 16)

            with sp.Fori(0, PAIRS // 2 - 1) as i:
                load_slots(i, 2)
                load_slots(i, 3)

            sp.wait_ge(S["yall"], 1)
            for n in range(NC):
                if n >= RING:
                    sp.wait_ge(S["fin"], done(n - RING + 1))
                for k in range(KTOP):
                    src = ybuf[k * NTOK + n * CT * P:k * NTOK + (n + 1) * CT * P, :]
                    sp.dma_start(yb[k][n % RING], src.rearrange("(t p) c -> p t c", p=P)).then_inc(s_yb[k][n], 16)
            for h in range(2):
                sp.wait_ge(s_out[h], NPART // 2 * 16)

        @block.gpsimd
        def _(pl):
            credit(pl, "c_const", "c_norm2", "c_yid", "pow1", "pow2", "ysent", "rows_sent")

            pl.memset(rw_raw[:], 0.0).then_inc(S["zeroed"], 1)
            cc = Chain(pl, S["c_const"], 0)
            cc.start(0)
            for a, value in ((ident, 0.0), (ident_b, 0.0), (ones_b, 1.0), (upper_b, 0.0), (mask_b, 0.0), (mhalf, -0.5),
                             (lower, 1.0), (padrow, 0.0)):
                cc.inc(pl.memset(a[:], value))
            for a, pattern, per_part in ((iota_e, [[1, E]], 0), (region0, [[REGION, E]], 0), (iota_s, [[1, SLOTS]], 0),
                                          (row_id, [[NTOK, KTOP], [P, NT]], 1)):
                cc.inc(pl.iota(a[:], pattern=pattern, base=0, channel_multiplier=per_part,
                               allow_small_or_imprecise_dtypes=True))
            cc.wait()
            for a in (ident, ident_b):
                cc.inc(pl.affine_select(out=a[:], in_=a[:], compare_op=ALU.not_equal, fill=1.0, base=0,
                                        pattern=[[-1, P]], channel_multiplier=1))
            for a, fill in ((upper_b, 1.0), (mask_b, MASKED)):
                cc.inc(pl.affine_select(out=a[:], in_=a[:], compare_op=ALU.is_ge, fill=fill, base=0,
                                        pattern=[[-1, P]], channel_multiplier=1))
            cc.inc(pl.affine_select(out=lower[:], in_=lower[:], compare_op=ALU.is_ge, fill=0.0, base=0,
                                    pattern=[[1, E], [-1, E]], channel_multiplier=0))
            cc.inc(pl.iota(padrow[:, C:C + 1].bitcast(I32), pattern=[[0, 1]], base=KTOP * NTOK, channel_multiplier=0))
            cc.wait()
            pl.nop().then_inc(S["const"], 1)

            def rstd_1():
                pl.tensor_tensor(rstd[:], veps[:], mhalf[:], ALU.pow).then_inc(S["pow1"], 1)

            def rstd_2(b):
                pl.wait_ge(S["st2"], done(b))
                alone(pl)
                bt = bass.ds(b * TB, TB)
                pl.tensor_tensor(rstd2_p[:, bt], veps2_p[:, bt], mhalf[:], ALU.pow).then_inc(S["pow2"], 1)

            pl.wait_ge(S["st1"], done(0))
            rstd_1()
            with pl.Fori(0, B - 1) as b:
                pl.wait_ge(S["st1"], done(b + 1))
                rstd_1()
                rstd_2(b)
            rstd_2(B - 1)
            rstd_2(B)

            c2 = Chain(pl, S["c_norm2"], KTOP)

            def row_names(i, off):
                g, par = 2 * i + off, off % 2
                c2.start(g)
                for k in range(KTOP):
                    c2.inc(pl.tensor_copy(xrow[k][par][:, :, C].bitcast(I32), row_id[:, k, bass.ds(g * GT, GT)]))
                c2.end()

            def send(i, off):
                g, par = 2 * i + off, off % 2
                pl.wait_ge(S["row1"], done(KTOP * g + 1))
                pl.wait_ge(S["rt2"], done(g))
                alone(pl)
                for t in range(GT):
                    for k in range(KTOP):
                        pl.indirect_dma_start(
                            out=xbuf, out_offset=bass.IndirectOffsetOnAxis(ap=pos[par][:, k, t:t + 1], axis=0),
                            in_=xrow[k][par][:, t, :], in_offset=None).then_inc(s_rows[par], 16)

            def sent(i, off):
                pl.wait_ge(s_rows[off % 2], (i + off // 2 + 1) * GT * KTOP * 16)
                alone(pl)
                pl.sem_inc(S["rows_sent"], 1)

            row_names(0, 0)
            row_names(0, 1)
            send(0, 0)
            send(0, 1)
            with pl.Fori(0, NG // 2 - 1) as i:
                for off in range(2):
                    sent(i, off)
                    row_names(i, off + 2)
                    send(i, off + 2)

            c3 = Chain(pl, S["c_yid"], 2)

            def send_y(i, off):
                p, par = 2 * i + off, off % 2
                c3.start(p)
                pl.wait_ge(S["emeta"], done(p))
                for k in range(2):
                    c3.inc(pl.tensor_copy(yid[2 * par + k][:], meta[:, bass.ds(2 * p + k, 1), 0].bitcast(I32)))
                c3.end()
                for k in range(2):
                    q = 2 * par + k
                    pl.wait_ge(S["eyout"], done(2 * p + k))
                    alone(pl)
                    pl.indirect_dma_start(out=ybuf, out_offset=bass.IndirectOffsetOnAxis(ap=yid[q][:], axis=0),
                                          in_=yrow[q][:], in_offset=None, bounds_check=KTOP * NTOK - 1,
                                          oob_is_err=False).then_inc(s_yw[q], 16)

            def sent_y(i, off):
                for k in range(2):
                    pl.wait_ge(s_yw[2 * (off % 2) + k], (i + off // 2 + 1) * 16)
                pl.nop().then_inc(S["ysent"], 1)

            send_y(0, 0)
            with pl.Fori(0, PAIRS // 2 - 1) as i:
                send_y(i, 1)
                sent_y(i, 0)
                send_y(i, 2)
                sent_y(i, 1)
            send_y(PAIRS // 2 - 1, 1)
            sent_y(PAIRS // 2 - 1, 0)
            sent_y(PAIRS // 2 - 1, 1)
            pl.nop().then_inc(S["yall"], 1)

        @block.scalar
        def _(act):
            credit(act, "c_n2", "smhi", "whi", "wfhi", "fhi", "prob", "pThi", "norm2", "row1", "t2hi", "lthi", "tanh",
                   "silu", "hhi", "yThi", "xhi", "esilu", "ehhi", "ylo")

            def normalise(b, first, last):
                if first == 0:
                    act.wait_ge(S["shift1"], done(b - 1))
                    act.wait_ge(S["fill"], done(6 * b - 3))
                    alone(act)
                for t in range(first, last):
                    act.activation(xn[:, t, :], tile_of(x_all, b * TB + t), ACT.Identity,
                                   bias=shift[:, t:t + 1], scale=rstd[:, t:t + 1]).then_inc(S["norm1"], 1)

            for n, factor in enumerate((1.0, SCALE, 1.0)):
                act.wait_ge(S["smT"], done(0))
                act.activation(sm_hi[:, n * C:(n + 1) * C], bank(7, C, n * C), ACT.Copy, scale=factor).then_inc(S["smhi"], 1)
            for n in range(NSH):
                act.wait_ge(S["wT"], done(n))
                act.activation(w_parts[:, n, :, 0, :], blocks(bank(2 + 2 * n, WCOLS)), ACT.Copy).then_inc(S["whi"], 1)

            def wf_hi(b, j):
                act.wait_ge(S["wfT"], done(4 * b + j))
                alone(act)
                act.activation(routed_half(b, j, 0), blocks(bank(7, HBLK * P)), ACT.Copy).then_inc(S["wfhi"], 1)

            def fill_hi(b, f):
                act.wait_ge(S["fill"], done(6 * b + f))
                dst = (xT_hi, yT_hi, v_hi)[f // 2]
                if f < 4:
                    act.wait_ge(S["score"], done(TB * b - 1))
                else:
                    act.wait_ge(S["pv"], done(TB * b - 1))
                act.activation(dst[:, f % 2 * 512:f % 2 * 512 + 512], bank(FILL_BANK[f]), ACT.Copy).then_inc(S["fhi"], 1)

            def exp(b, k):
                i, n = ORDER[k], TB * b + k
                act.wait_ge(S["nmax"], done(n))
                act.wait_ge(S["pT"], done(NCH * b + (CH[k - 1] if k else 0) - 1))
                act.wait_ge(S["rinv"], done(n - 2))
                act.activation(prob[k % 2][:, 0:(i + 1) * P], bank(2 * (k % 2), (i + 1) * P), ACT.Exp,
                               bias=nmax[:, i:i + 1], accum_out=rsum[:, i:i + 1]).then_inc(S["prob"], 1)

            def pT_split(b, k, h):
                bk, j0, j1 = chunks(k)[h]
                act.wait_ge(S["pT"], done(NCH * b + CH[k] + h))
                act.wait_ge(S["pv"], done(TB * b + k - 2))
                act.activation(pT_hi[k % 2][:, j0 * P:j1 * P], bank(bk, (j1 - j0) * P), ACT.Copy).then_inc(S["pThi"], 1)

            c_n2 = Chain(act, S["c_n2"], GT)

            def normalise2(i, off, first=0, last=GT):
                g, par = 2 * i + off, off % 2
                if first == 0:
                    c_n2.start(g)
                for t in range(first, last):
                    n = bass.ds(g * GT + t, 1)
                    c_n2.inc(act.activation(xn[:, par * GT + t, :], tile_of(x_all, g * GT + t), ACT.Identity,
                                            bias=shift2[:, n], scale=rstd2[:, n]))
                if last == GT:
                    c_n2.end()
                    act.nop().then_inc(S["norm2"], 1)

            def t2_hi(i, off, bk=6):
                g = 2 * i + off
                act.wait_ge(S["t2"], done(g))
                act.activation(x2T_hi[off % 2][:], bank(bk), ACT.Copy).then_inc(S["t2hi"], 1)

            def first_exps(b):
                exp(b, 0)
                fill_hi(b, 4)
                exp(b, 1)
                fill_hi(b, 5)

            def batch_act(b, more):
                pT_split(b, 0, 0)
                wf_hi(b, 0)
                for k in range(2, TB):
                    for h in range(len(chunks(k - 1))):
                        pT_split(b, k - 1, h)
                    if k <= 3:
                        wf_hi(b, k - 1)
                    exp(b, k)
                    if k == 4:
                        wf_hi(b, k - 1)
                    if more and 5 <= k <= 6:
                        normalise(b + 1, 4 * (k - 5), 4 * (k - 4))
                    if not more and k == 5:
                        act.wait_ge(S["shift2"], 1)
                        normalise2(0, 0)
                    if not more and k == 6:
                        normalise2(0, 1)
                if more:
                    fill_hi(b + 1, 0)
                else:
                    t2_hi(0, 0, 7)
                pT_split(b, TB - 1, 0)
                if more:
                    fill_hi(b + 1, 1)
                pT_split(b, TB - 1, 1)
                if more:
                    fill_hi(b + 1, 2)
                    fill_hi(b + 1, 3)
                    first_exps(b + 1)

            for f in range(4):
                fill_hi(0, f)
            first_exps(0)
            with act.Fori(0, B - 1) as b:
                batch_act(b, True)
            batch_act(B - 1, False)

            def rows(i, off):
                g, par = 2 * i + off, off % 2
                act.wait_ge(S["rows_sent"], done(g - 2))
                alone(act)
                for k in range(KTOP):
                    act.activation(xrow[k][par][:, :, 0:C], xn[:, par * GT:(par + 1) * GT, :], ACT.Copy).then_inc(S["row1"], 1)

            def lt_bias(i, off, bk=6):
                g = 2 * i + off
                act.wait_ge(S["lt"], done(g))
                act.wait_ge(S["r3"], done(g - 1))
                act.activation(logitT[:], bank(bk)[0:E, :], ACT.Identity, bias=bias_col[:]).then_inc(S["lthi"], 1)

            def unit_silu(g, u):
                n = 4 * g + u
                act.wait_ge(S["gu"], done(n))
                act.wait_ge(S["mul"], done(n - 2))
                act.activation(sil[u % 2][:], bank(2 * (u % 2)), ACT.Silu).then_inc(S["silu"], 1)

            def unit_hi(g, u):
                n = 4 * g + u
                act.wait_ge(S["mul"], done(n))
                act.wait_ge(S["yT"], done(n - 2))
                act.activation(hT_hi[u % 2][:], hid[u % 2][:], ACT.Copy).then_inc(S["hhi"], 1)

            def weights(g):
                act.wait_ge(S["rt1"], done(g))
                act.activation(gapt[:], gap[:], ACT.Tanh, scale=0.5).then_inc(S["tanh"], 1)

            def shared_copy(i, off):
                g = 2 * i + off
                act.wait_ge(S["yT"], done(4 * g + 3))
                act.wait_ge(S["back"], done(g - 1))
                act.activation(shT[:], bank(4), ACT.Copy).then_inc(S["yThi"], 1)

            def shared_act(i, off, route, norm):
                g = 2 * i + off
                unit_silu(g, 2)
                if route:
                    t2_hi(i, off + 1)
                unit_hi(g, 2)
                unit_silu(g, 3)
                if route:
                    lt_bias(i, off + 1)
                unit_hi(g, 3)
                if route:
                    unit_silu(g + 1, 0)
                    rows(i, off + 1)
                    unit_hi(g + 1, 0)
                shared_copy(i, off)
                if route:
                    weights(g + 1)
                    unit_silu(g + 1, 1)
                if norm:
                    normalise2(i, off + 2, 0, 2)
                if route:
                    unit_hi(g + 1, 1)
                if norm:
                    normalise2(i, off + 2, 2, GT)

            lt_bias(0, 0, 1)
            rows(0, 0)
            unit_silu(0, 0)
            unit_hi(0, 0)
            weights(0)
            unit_silu(0, 1)
            unit_hi(0, 1)
            act.wait_ge(S["shift2"], 2)
            with act.Fori(0, NG // 2 - 1) as i:
                shared_act(i, 0, True, True)
                shared_act(i, 1, True, True)
            shared_act(NG // 2 - 1, 0, True, False)
            shared_act(NG // 2 - 1, 1, False, False)

            def x_hi(i, off):
                p, par = 2 * i + off, off % 2
                act.wait_ge(S["tx"], done(p))
                act.wait_ge(S["eh"], done(p - 2))
                act.activation(gT_hi[par][:], bank(4, 2 * P), ACT.Copy).then_inc(S["xhi"], 1)

            def e_silu(i, off):
                p, par = 2 * i + off, off % 2
                act.wait_ge(S["eh"], done(p))
                act.wait_ge(S["emul"], done(p - 2))
                act.activation(sil[par][:].rearrange("p (s h) -> p s h", s=2),
                               halves(ps[:, 1024 * par:1024 * par + 1024], 0),
                               ACT.Silu).then_inc(S["esilu"], 1)

            def h_hi(i, off):
                p, par = 2 * i + off, off % 2
                act.wait_ge(S["eth"], done(p))
                act.wait_ge(S["ey"], done(2 * p - 3))
                act.activation(hT_hi[par][:], bank(5), ACT.Copy).then_inc(S["ehhi"], 1)

            def y_small(i, off, k):
                p, par = 2 * i + off, off % 2
                act.wait_ge(S["ey"], done(2 * p + k))
                act.wait_ge(S["eyout"], done(2 * p + k - 3))
                act.wait_ge(S["emeta"], done(p))
                alone(act)
                act.activation(ylo[2 * par + k][:], bank(6 + k, P, P), ACT.Copy,
                               scale=meta[:, bass.ds(2 * p + k, 1), 1]).then_inc(S["ylo"], 1)

            def e_step(i, off, y1=True, h=True, x=True, y0=True, up=True):
                if y1:
                    y_small(i, off - 2, 1)
                if h:
                    h_hi(i, off)
                if x:
                    x_hi(i, off + 3)
                if y0:
                    y_small(i, off - 1, 0)
                if up:
                    e_silu(i, off + 2)

            x_hi(0, 0)
            x_hi(0, 1)
            e_silu(0, 0)
            x_hi(0, 2)
            e_silu(0, 1)
            e_step(0, 0, y1=False, y0=False)
            e_step(0, 1, y1=False)
            L = PAIRS // 2
            with act.Fori(1, L - 2) as i:
                e_step(i, 0)
                e_step(i, 1)
            e_step(L - 2, 0)
            e_step(L - 2, 1, x=False)
            e_step(L - 1, 0, x=False, up=False)
            e_step(L - 1, 1, x=False, up=False)
            e_step(L, 0, h=False, x=False, up=False)
            e_step(L, 1, h=False, x=False, y0=False, up=False)

            for m, (n, t0, t1) in enumerate(PARTS):
                act.wait_ge(S["fin"], done(m))
                t = slice(n * CT + t0, n * CT + t1)
                act.dma_start(out_rows[:, t, :], x_all[:, t, :]).then_inc(s_out[m % 2], 16)

        @block.vector
        def _(ve):
            credit(ve, "c_st1", "c_st2", "c_agg", "c_cnt", "c_rt1", "c_rt2", "c_tab", "c_tab2", "c_fin")
            credit(ve, "smlo", "wlo", "wflo", "st1", "shift1", "norm1", "flo", "nmax", "pTlo", "rinv", "x2", "st2",
                   "t2lo", "rt1", "rt2", "mul", "hlo", "addb", "xlo", "emeta", "emul", "ehlo", "eyout", "fin")

            c1 = Chain(ve, S["c_st1"], 2 * TB)

            def stats1(b, first, last):
                if first == 0:
                    c1.start(b)
                for t in range(first, last):
                    c1.inc(ve.bn_stats(stats[:, t, :], tile_of(x_all, b * TB + t)))

            def aggr1(b):
                c1.wait()
                alone(ve)
                for t in range(TB):
                    c1.inc(ve.bn_aggr(mv[:, t, :], stats[:, t, :]))
                c1.end()
                ve.tensor_scalar(veps[:], mv[:, :, 1], EPS, None, ALU.add).then_inc(S["st1"], 1)

            ve.memset(stats2[:], 1.0).then_inc(S["filled2"], 1)

            def shift_1(b):
                ve.wait_ge(S["pow1"], done(b))
                ve.scalar_tensor_tensor(out=shift[:], in0=mv[:, :, 0], scalar=-1.0, in1=rstd[:], op0=ALU.mult,
                                        op1=ALU.mult).then_inc(S["shift1"], 1)

            ve.wait_ge(s_x0, 16)
            stats1(0, 0, TB)
            aggr1(0)
            ve.wait_ge(S["smhi"], done(2))
            for n, factor in enumerate((1.0, SCALE, 1.0)):
                c = slice(n * C, (n + 1) * C)
                ve.scalar_tensor_tensor(out=sm_lo[:, c], in0=bank(7, C, n * C), scalar=factor, in1=sm_hi[:, c].bitcast(F32),
                                        op0=ALU.mult, op1=ALU.subtract).then_inc(S["smlo"], 1)

            ve.wait_ge(S["pow1"], done(0))
            for t in range(TB):
                ve.tensor_scalar(xn[:, t, :], x_all[:, t, :], mv[:, t, 0:1], rstd[:, t:t + 1],
                                 ALU.subtract, ALU.mult).then_inc(S["norm1"], 1)

            def shared_lo(n):
                ve.wait_ge(S["whi"], done(n))
                ve.tensor_tensor(w_parts[:, n, :, 1, :], blocks(bank(2 + 2 * n, WCOLS)), w_parts[:, n, :, 0, :].bitcast(F32),
                                 ALU.subtract).then_inc(S["wlo"], 1)

            def wf_lo(b, j):
                ve.wait_ge(S["wfhi"], done(4 * b + j))
                ve.tensor_tensor(routed_half(b, j, 1), blocks(bank(7, HBLK * P)), routed_half(b, j, 0).bitcast(F32),
                                 ALU.subtract).then_inc(S["wflo"], 1)

            def fill_lo(b, f):
                src_hi = (xT_hi, yT_hi, v_hi)[f // 2]
                dst = (xT_lo, yT_lo, v_lo)[f // 2]
                ve.wait_ge(S["fhi"], done(6 * b + f))
                c = slice(f % 2 * 512, f % 2 * 512 + 512)
                ve.tensor_tensor(dst[:, c], bank(FILL_BANK[f]), src_hi[:, c].bitcast(F32), ALU.subtract).then_inc(S["flo"], 1)

            def invert(b, k):
                i = ORDER[k]
                ve.reciprocal(rinv[:, i:i + 1], rsum[:, i:i + 1]).then_inc(S["rinv"], 1)

            def row_max(b, k):
                i, n = ORDER[k], TB * b + k
                ve.wait_ge(S["score"], done(n))
                ve.wait_ge(S["prob"], done(n - 2))
                ve.tensor_reduce(nmax[:, i:i + 1], bank(2 * (k % 2), (i + 1) * P), AXX, ALU.max,
                                 negate=True).then_inc(S["nmax"], 1)

            def pT_rest(b, k, h):
                bk, j0, j1 = chunks(k)[h]
                ve.wait_ge(S["pThi"], done(NCH * b + CH[k] + h))
                ve.tensor_tensor(pT_lo[k % 2][:, j0 * P:j1 * P], bank(bk, (j1 - j0) * P),
                                 pT_hi[k % 2][:, j0 * P:j1 * P].bitcast(F32), ALU.subtract).then_inc(S["pTlo"], 1)

            def add_attn(b, k):
                i, n = ORDER[k], TB * b + k
                ve.wait_ge(S["pv"], done(n))
                ve.wait_ge(S["rinv"], done(n))
                xt = tile_of(x_all, TB * b + i)
                ve.scalar_tensor_tensor(out=xt, in0=bank(6, P), scalar=rinv[:, i:i + 1], in1=xt,
                                        op0=ALU.mult, op1=ALU.add).then_inc(S["x2"], 1)

            c_x2 = Chain(ve, S["c_st2"], TB)
            c_agg = Chain(ve, S["c_agg"], TB)

            def stats_2(b, k):
                ve.wait_ge(S["x2"], done(TB * b + k))
                alone(ve)
                c_x2.inc(ve.bn_stats(stats2[:, ORDER[k], :], tile_of(x_all, TB * b + ORDER[k])))

            def aggr_2(b):
                c_agg.start(b)
                ve.wait_ge(S["st2"], done(b - 1))
                c_x2.wait()
                alone(ve)
                for t in range(TB):
                    c_agg.inc(ve.bn_aggr(mv2[:, t, :], stats2[:, t, :]))
                c_agg.end()
                bt = bass.ds(TB * b, TB)
                ve.tensor_copy(mean2_p[:, bt], mv2[:, :, 0])
                ve.tensor_scalar(veps2_p[:, bt], mv2[:, :, 1], EPS, None, ALU.add).then_inc(S["st2"], 1)

            def shift_2(first, last):
                ve.wait_ge(S["pow2"], done(last // TB))
                t = slice(first, last)
                ve.scalar_tensor_tensor(out=shift2[:, t], in0=mean2[:, t], scalar=-1.0, in1=rstd2[:, t], op0=ALU.mult,
                                        op1=ALU.mult).then_inc(S["shift2"], 1)

            def t2_lo(i, off, bk=6):
                g = 2 * i + off
                ve.wait_ge(S["t2hi"], done(g))
                ve.tensor_tensor(x2T_lo[off % 2][:], bank(bk), x2T_hi[off % 2][:].bitcast(F32),
                                 ALU.subtract).then_inc(S["t2lo"], 1)

            def batch_dve(b, more):
                c_x2.start(b)
                for k in range(1, TB):
                    if k >= 2:
                        row_max(b, k)
                    if k == 2:
                        add_attn(b, 0)
                        wf_lo(b, 1)
                    for h in range(len(chunks(k - 1))):
                        pT_rest(b, k - 1, h)
                    invert(b, k - 1)
                    if k >= 3:
                        add_attn(b, k - 2)
                    if k <= 4 and k != 2:
                        wf_lo(b, k - 1)
                    if more and k == 5:
                        shift_1(b + 1)
                    if k == 5:
                        aggr_2(b)
                        stats_2(b, 0)
                        stats_2(b, 1)
                    if k >= 5:
                        stats_2(b, k - 3)
                    if more and k <= 3:
                        stats1(b + 1, 3 * (k - 1), min(3 * k, TB))
                    if more and k == 4:
                        aggr1(b + 1)
                    if not more and k == 3:
                        shift_2(0, (B - 2) * TB)
                if more:
                    fill_lo(b + 1, 0)
                else:
                    t2_lo(0, 0, 7)
                pT_rest(b, TB - 1, 0)
                if more:
                    fill_lo(b + 1, 1)
                pT_rest(b, TB - 1, 1)
                invert(b, TB - 1)
                add_attn(b, TB - 2)
                if more:
                    fill_lo(b + 1, 2)
                    fill_lo(b + 1, 3)
                    row_max(b + 1, 0)
                    add_attn(b, TB - 1)
                    for k in range(TB - 3, TB):
                        stats_2(b, k)
                    row_max(b + 1, 1)
                    fill_lo(b + 1, 4)
                    fill_lo(b + 1, 5)

            shared_lo(0)
            fill_lo(0, 0)
            fill_lo(0, 1)
            shared_lo(1)
            fill_lo(0, 2)
            fill_lo(0, 3)
            row_max(0, 0)
            row_max(0, 1)
            fill_lo(0, 4)
            fill_lo(0, 5)
            ve.wait_ge(s_x1, 16)
            ve.wait_ge(S["filled2"], 1)
            with ve.Fori(0, B - 1) as b:
                batch_dve(b, True)
            batch_dve(B - 1, False)

            c_rt1 = Chain(ve, S["c_rt1"], 2 * GT + 3)
            c_rt2 = Chain(ve, S["c_rt2"], 8)

            def route1(i, off):
                g = 2 * i + off
                c_rt1.start(g)
                ve.wait_ge(S["r3"], done(g))
                alone(ve)
                for t in range(GT):
                    c_rt1.inc(ve.max(top[:, t, :], bank(7, E, t * E)))
                c_rt1.wait()
                alone(ve)
                for t in range(GT):
                    c_rt1.inc(ve.max_index(topi[:, t, :], top[:, t, :], bank(7, E, t * E)))
                c_rt1.wait()
                c_rt1.link(ve.tensor_copy(topf[:], topi[:, :, 0:KTOP].rearrange("p t k -> p k t")))
                c_rt1.inc(ve.tensor_tensor(hot[:], iota_e[:].unsqueeze(1).unsqueeze(1).broadcast_to([P, KTOP, GT, E]),
                                           topf[:].unsqueeze(3).broadcast_to([P, KTOP, GT, E]), ALU.is_equal))
                c_rt1.inc(ve.tensor_tensor(gap[:], top[:, :, 0], top[:, :, 1], ALU.subtract))
                c_rt1.end()
                ve.tensor_tensor(hot_b[:], hot[:, 0], hot[:, 1], ALU.add).then_inc(S["rt1"], 1)

            def route2(i, off):
                g, par = 2 * i + off, off % 2
                c_rt2.start(g)
                ve.wait_ge(S["rk"], done(g))
                ve.wait_ge(S["tanh"], done(g))
                ve.wait_ge(S["rows_sent"], done(g - 2))
                c_rt2.inc(ve.tensor_tensor(place[:], bank(7, GT * E, 64).rearrange("p (t e) -> p t e", e=E),
                                           count[:].unsqueeze(1).broadcast_to([P, GT, E]), ALU.add))
                c_rt2.link(ve.tensor_reduce(added[:], bank(7, GT * E, 128).rearrange("p (t e) -> p e t", e=E), AXX, ALU.add))
                c_rt2.inc(ve.tensor_tensor(count[:], count[:], added[:], ALU.add))
                c_rt2.link(ve.tensor_tensor(picked[:], place[:].unsqueeze(1).broadcast_to([P, KTOP, GT, E]), hot[:], ALU.mult))
                c_rt2.link(ve.tensor_reduce(posf[:], picked[:], AXX, ALU.add))
                c_rt2.inc(ve.tensor_copy(pos[par][:], posf[:]))
                for k in range(KTOP):
                    c_rt2.inc(ve.tensor_scalar(xrow[k][par][:, :, C + 1], gapt[:], 0.5 - k, 0.5, ALU.mult, ALU.add))
                c_rt2.end()
                ve.nop().then_inc(S["rt2"], 1)

            def unit_mul(g, u):
                n = 4 * g + u
                ve.wait_ge(S["silu"], done(n))
                ve.wait_ge(S["hhi"], done(n - 2))
                ve.tensor_tensor(hid[u % 2][:], sil[u % 2][:], bank(2 * (u % 2) + 1), ALU.mult).then_inc(S["mul"], 1)

            def unit_lo(g, u):
                ve.wait_ge(S["hhi"], done(4 * g + u))
                ve.tensor_tensor(hT_lo[u % 2][:], hid[u % 2][:], hT_hi[u % 2][:].bitcast(F32),
                                 ALU.subtract).then_inc(S["hlo"], 1)

            c_tab = Chain(ve, S["c_tab"], 10)

            def expert_ends():
                c, rows, tiles, ends = c_tab, t8[0], t8[1], t8[2]
                c.start(0)
                c.link(ve.tensor_tensor(rows[:], count[0:1, :], region0[0:1, :], ALU.subtract))
                c.link(ve.tensor_scalar(t8i[:], rows[:], float(P - 1), None, ALU.add))
                c.link(ve.tensor_scalar(t8i[:], t8i[:], 7, None, ALU.arith_shift_right))
                c.link(ve.tensor_copy(tiles[:], t8i[:]))
                c.inc(ve.tensor_scalar(rows[:], tiles[:], -float(P), float(REGION), ALU.mult, ALU.add))
                c.link(ve.tensor_tensor(t64[:], lower[:], tiles[:].unsqueeze(1).broadcast_to([1, E, E]), ALU.mult))
                c.inc(ve.tensor_reduce(ends[:], t64[:], AXX, ALU.add))

            def ended():
                c_tab.wait()
                c_tab.inc(ve.tensor_tensor(past[:], iota_s[:].unsqueeze(2).broadcast_to([1, SLOTS, E]),
                                           t8[2][:].unsqueeze(1).broadcast_to([1, SLOTS, E]), ALU.is_ge))

            def slot_rows():
                c = c_tab
                c.wait()
                c.link(ve.tensor_tensor(past2[:], past[:], t8[0][:].unsqueeze(1).broadcast_to([1, SLOTS, E]), ALU.mult))
                c.link(ve.tensor_reduce(slot_t[:], past2[:], AXX, ALU.add))
                ve.scalar_tensor_tensor(out=slot_ri[:], in0=iota_s[:], scalar=float(P), in1=slot_t[:],
                                        op0=ALU.mult, op1=ALU.add).then_inc(S["tabr"], 1)

            def step_tables():
                c = Chain(ve, S["c_tab2"], 8)
                c.start(0)
                c.link(ve.tensor_reduce(slot_e[:], past[:], AXX, ALU.add))
                c.inc(ve.tensor_scalar(slot_w[:], slot_e[:], float(E - 1), None, ALU.min))
                c.link(ve.memset(step_w[:], 0.0))
                w2v = slot_w[:].rearrange("o (p k) -> o p k", k=2)
                for shift_by, k, factor in ((0, 0, 1.0), (0, 1, 8.0), (3, 0, 64.0), (4, 1, 512.0)):
                    sw = step_w[:, shift_by:shift_by + PAIRS]
                    c.link(ve.scalar_tensor_tensor(out=sw, in0=w2v[:, :, k], scalar=factor, in1=sw,
                                                   op0=ALU.mult, op1=ALU.add))
                by_two = step_w[:].rearrange("o (i h) -> o i h", h=2)
                c.link(ve.scalar_tensor_tensor(out=step_wi[:], in0=by_two[:, :, 1], scalar=4096.0, in1=by_two[:, :, 0],
                                               op0=ALU.mult, op1=ALU.add))
                c.end()
                ve.nop().then_inc(S["tab"], 1)

            def add_shared(i, off):
                g = 2 * i + off
                ve.wait_ge(S["back"], done(g))
                xg4 = x_all[:, bass.ds(g * GT, GT), :]
                ve.tensor_tensor(xg4, xg4, bank(5).rearrange("p (t c) -> p t c", c=C), ALU.add).then_inc(S["addb"], 1)

            def shared_dve(i, off, route, last=False):
                g = 2 * i + off
                unit_mul(g, 2)
                if route:
                    t2_lo(i, off + 1)
                else:
                    expert_ends()
                unit_lo(g, 2)
                unit_mul(g, 3)
                if not route:
                    ended()
                unit_lo(g, 3)
                if not route:
                    slot_rows()
                if route:
                    unit_mul(g + 1, 0)
                    route1(i, off + 1)
                    unit_lo(g + 1, 0)
                    unit_mul(g + 1, 1)
                    route2(i, off + 1)
                    if last:
                        ve.tensor_copy(padpos[:], count[0:1, :]).then_inc(S["padpos"], 1)
                    unit_lo(g + 1, 1)
                else:
                    step_tables()
                add_shared(i, off)

            ve.wait_ge(S["const"], 1)
            c_cnt = Chain(ve, S["c_cnt"], 1)
            c_cnt.start(0)
            c_cnt.link(ve.tensor_copy(count[:], region0[:]))
            route1(0, 0)
            add_attn(B - 1, TB - 1)
            for k in range(TB - 3, TB):
                stats_2(B - 1, k)
            aggr_2(B)
            unit_mul(0, 0)
            unit_lo(0, 0)
            shift_2((B - 2) * TB, NT)
            unit_mul(0, 1)
            route2(0, 0)
            unit_lo(0, 1)
            with ve.Fori(0, NG // 2 - 1) as i:
                shared_dve(i, 0, True)
                shared_dve(i, 1, True)
            shared_dve(NG // 2 - 1, 0, True, last=True)
            shared_dve(NG // 2 - 1, 1, False)

            def x_lo(i, off):
                p, par = 2 * i + off, off % 2
                for k in range(2):
                    ve.wait_ge(s_xg[2 * par + k], (i + off // 2 + 1) * 16)
                ve.tensor_copy(meta[:, bass.ds(2 * p, 2), :], xg[:, 2 * par:2 * par + 2, C:C + 2]).then_inc(S["emeta"], 1)
                ve.wait_ge(S["xhi"], done(p))
                ve.tensor_tensor(gT_lo[par][:], bank(4, 2 * P), gT_hi[par][:].bitcast(F32), ALU.subtract).then_inc(S["xlo"], 1)

            def e_mul(i, off):
                p, par = 2 * i + off, off % 2
                ve.wait_ge(S["esilu"], done(p))
                ve.wait_ge(S["eth"], done(p - 2))
                ve.tensor_tensor(hid[par][:].rearrange("p (s h) -> p s h", s=2), sil[par][:].rearrange("p (s h) -> p s h", s=2),
                                 halves(ps[:, 1024 * par:1024 * par + 1024], 1), ALU.mult).then_inc(S["emul"], 1)

            def h_lo(i, off):
                p, par = 2 * i + off, off % 2
                ve.wait_ge(S["ehhi"], done(p))
                ve.tensor_tensor(hT_lo[par][:], bank(5), hT_hi[par][:].bitcast(F32), ALU.subtract).then_inc(S["ehlo"], 1)

            def y_out(i, off, k):
                p, par = 2 * i + off, off % 2
                ve.wait_ge(S["ylo"], done(2 * p + k))
                if k == 0:
                    ve.wait_ge(S["ysent"], done(p - 2))
                    ve.wait_ge(S["emeta"], done(p))
                ve.scalar_tensor_tensor(out=yrow[2 * par + k][:], in0=bank(6 + k, P),
                                        scalar=meta[:, bass.ds(2 * p + k, 1), 1], in1=ylo[2 * par + k][:],
                                        op0=ALU.mult, op1=ALU.add).then_inc(S["eyout"], 1)

            def e_step(i, off, y1=True, h=True, x=True, y0=True, up=True):
                if y1:
                    y_out(i, off - 2, 1)
                if h:
                    h_lo(i, off)
                if x:
                    x_lo(i, off + 3)
                if y0:
                    y_out(i, off - 1, 0)
                if up:
                    e_mul(i, off + 2)

            x_lo(0, 0)
            x_lo(0, 1)
            e_mul(0, 0)
            x_lo(0, 2)
            e_mul(0, 1)
            e_step(0, 0, y1=False, y0=False)
            e_step(0, 1, y1=False)
            L = PAIRS // 2
            with ve.Fori(1, L - 2) as i:
                e_step(i, 0)
                e_step(i, 1)
            e_step(L - 2, 0)
            e_step(L - 2, 1, x=False)
            e_step(L - 1, 0, x=False, up=False)
            e_step(L - 1, 1, x=False, up=False)
            e_step(L, 0, h=False, x=False, up=False)
            e_step(L, 1, h=False, x=False, y0=False, up=False)

            c_fin = Chain(ve, S["c_fin"], NPART)
            c_fin.start(0)
            for n, t0, t1 in PARTS:
                xc = x_all[:, n * CT + t0:n * CT + t1, :]
                ve.wait_ge(s_yb[0][n], 16)
                c_fin.link(ve.tensor_tensor(xc, xc, yb[0][n % RING][:, t0:t1], ALU.add))
                ve.wait_ge(s_yb[1][n], 16)
                ve.tensor_tensor(xc, xc, yb[1][n % RING][:, t0:t1], ALU.add).then_inc(S["fin"], 1)

        @block.tensor
        def _(pe):
            credit(pe, "wfT", "wT", "smT", "score", "pT", "pv", "fill", "t2", "lt", "r3", "rk", "gu", "yT", "back",
                   "tx", "eh", "eth", "ey")

            def product(dst, a_hi, a_lo, b_hi, b_lo, start=True, stop=True):
                pe.matmul(dst, a_lo, b_hi, start=start, stop=False)
                pe.matmul(dst, a_hi, b_lo, start=False, stop=False)
                return pe.matmul(dst, a_hi, b_hi, start=False, stop=stop)

            pe.wait_ge(S["const"], 1)
            pe.wait_ge(s_small, 5 * 16)
            pe.transpose(bank(7, P), wqkv[:, 2, :], ident[:])
            pe.matmul(bank(7, P, P), wqkv[:, 0, :], wqkv[:, 1, :], start=True, stop=True)
            pe.transpose(bank(7, P, 2 * P), rw_raw[:], ident[:]).then_inc(S["smT"], 1)
            wv_hi, wv_lo = sm_hi[:, 0:C], sm_lo[:, 0:C]
            m_hi, m_lo = sm_hi[:, C:2 * C], sm_lo[:, C:2 * C]
            r_hi, r_lo = sm_hi[:, 2 * C:SM], sm_lo[:, 2 * C:SM]

            for n in range(NSH):
                pe.wait_ge(s_raw[n], 3 * 16)
                for j in range(WBLK):
                    last = pe.transpose(bank(2 + 2 * n, P, j * P), raw[n][:, j, :], ident[:])
                last.then_inc(S["wT"], 1)

            def wf_transpose(b, j):
                pe.wait_ge(s_raw[j // 2], (b + 2) * 3 * 16)
                pe.wait_ge(S["wflo"], done(4 * b + j - 1))
                for m in range(3):
                    last = pe.transpose(bank(7, P, m * P), raw[j // 2][:, j % 2 * 3 + m, :], ident[:])
                last.then_inc(S["wfT"], 1)

            def fill(b, f):
                dst = bank(FILL_BANK[f])
                if f < 4:
                    pe.wait_ge(S["flo"], done(6 * b + f - (3 if f < 2 else 2)))
                else:
                    pe.wait_ge(S["pTlo"], done(NCH * b - 1))
                if f < 2:
                    pe.wait_ge(S["norm1"], done(TB * b + 4 * f + 3))
                    for j in range(4):
                        last = pe.transpose(dst[:, j * P:(j + 1) * P], xn[:, 4 * f + j, :], ident[:])
                elif f < 4:
                    c = slice(f % 2 * 512, f % 2 * 512 + 512)
                    last = product(dst, m_hi, m_lo, xT_hi[:, c], xT_lo[:, c])
                else:
                    for j in range(4):
                        c = slice((f % 2 * 4 + j) * P, (f % 2 * 4 + j + 1) * P)
                        last = product(dst[:, j * P:(j + 1) * P], xT_hi[:, c], xT_lo[:, c], wv_hi, wv_lo)
                last.then_inc(S["fill"], 1)

            def score(b, k):
                i, n = ORDER[k], TB * b + k
                pe.wait_ge(S["prob"], done(n - 2))
                if k < 2:
                    pe.wait_ge(S["flo"], done(6 * b + 2 + k))
                q = slice(i * P, (i + 1) * P)
                width = (i + 1) * P
                base = 2 * (k % 2)
                for c0 in range(0, width, 512):
                    c1 = min(c0 + 512, width)
                    product(bank(base, c1 - c0, c0), yT_hi[:, q], yT_lo[:, q], xT_hi[:, c0:c1], xT_lo[:, c0:c1],
                            stop=c1 < width)
                pe.matmul(bank(base, P, i * P), ident_b[:], mask_b[:], start=False, stop=True).then_inc(S["score"], 1)

            def p_transpose(b, k, h):
                bk, j0, j1 = chunks(k)[h]
                if h == 0:
                    pe.wait_ge(S["prob"], done(TB * b + k))
                if k == 1:
                    pe.wait_ge(S["flo"], done(6 * b + 4 + h))
                pe.wait_ge(S["pTlo"], done(NCH * b + CH[k] + h - 3))
                for j in range(j0, j1):
                    last = pe.transpose(bank(bk, P, (j - j0) * P), prob[k % 2][:, j * P:(j + 1) * P], ident[:])
                last.then_inc(S["pT"], 1)

            def pv(b, k, h):
                bk, j0, j1 = chunks(k)[h]
                i = ORDER[k]
                pe.wait_ge(S["pTlo"], done(NCH * b + CH[k] + h))
                if h == 0:
                    pe.wait_ge(S["x2"], done(TB * b + k - 1))
                for j in range(j0, j1):
                    c = slice(j * P, (j + 1) * P)
                    last = product(bank(6, P), pT_hi[k % 2][:, c], pT_lo[k % 2][:, c], v_hi[:, c], v_lo[:, c],
                                   start=j == 0, stop=j == i)
                if j1 == i + 1:
                    last.then_inc(S["pv"], 1)

            def t2(i, off, bk=6):
                g, par = 2 * i + off, off % 2
                pe.wait_ge(S["norm2"], done(g))
                pe.wait_ge(S["lthi"], done(g - 1))
                for t in range(GT):
                    last = pe.transpose(bank(bk, P, t * P), xn[:, par * GT + t, :], ident[:])
                last.then_inc(S["t2"], 1)

            def logits_T(i, off, bk=6):
                g = 2 * i + off
                pe.wait_ge(S["t2lo"], done(g))
                product(bank(bk), r_hi, r_lo, x2T_hi[off % 2][:], x2T_lo[off % 2][:]).then_inc(S["lt"], 1)

            def batch_pe(b, more):
                for k in range(TB):
                    score(b, k)
                    if k == 1:
                        fill(b, 4)
                        fill(b, 5)
                    if k == TB - 1:
                        pe.wait_ge(S["wflo"], done(4 * b + 3))
                        if more:
                            fill(b + 1, 0)
                        else:
                            t2(0, 0, 7)
                    if k >= 1:
                        for h in range(len(chunks(k - 1))):
                            p_transpose(b, k - 1, h)
                    if 1 <= k <= 4:
                        wf_transpose(b, k - 1)
                    if k >= 2:
                        for h in range(len(chunks(k - 2))):
                            pv(b, k - 2, h)
                p_transpose(b, TB - 1, 0)
                if more:
                    pe.wait_ge(S["pTlo"], done(NCH * b + CH[TB - 2]))
                    fill(b + 1, 1)
                p_transpose(b, TB - 1, 1)
                pv(b, TB - 2, 0)
                if more:
                    fill(b + 1, 2)
                    fill(b + 1, 3)
                else:
                    pe.wait_ge(S["pTlo"], done(NCH * b + CH[TB - 2]))
                    logits_T(0, 0, 1)
                pv(b, TB - 1, 0)
                pv(b, TB - 1, 1)

            pe.wait_ge(S["smlo"], done(2))
            for f in range(4):
                fill(0, f)
            pe.wait_ge(S["wlo"], done(NSH - 1))
            with pe.Fori(0, B - 1) as b:
                batch_pe(b, True)
            batch_pe(B - 1, False)

            def logits(i, off):
                g = 2 * i + off
                pe.wait_ge(S["lthi"], done(g))
                pe.wait_ge(S["rt2"], done(g - 1))
                alone(pe)
                for t in range(GT):
                    last = pe.transpose(bank(7, E, t * E), logitT[:, t * P:(t + 1) * P], ident[0:E, 0:E])
                last.then_inc(S["r3"], 1)

            def ranks(i, off):
                g = 2 * i + off
                pe.wait_ge(S["rt1"], done(g))
                pe.wait_ge(S["rt2"], done(g - 1))
                hot2 = hot_b[:].rearrange("p t e -> p (t e)")
                pe.matmul(bank(7, GT * E, 64), upper_b[:], hot2, start=True, stop=False)
                for t in range(GT - 1):
                    pe.matmul(bank(7, (GT - 1 - t) * E, 64 + (t + 1) * E).rearrange("p (t e) -> p t e", e=E), ones_b[:],
                              hot_b[:, t:t + 1, :].broadcast_to([P, GT - 1 - t, E]), start=False, stop=t == GT - 2)
                pe.matmul(bank(7, GT * E, 128), ones_b[:], hot2, start=True, stop=True).then_inc(S["rk"], 1)

            def unit_up(i, off, u):
                g = 2 * i + off
                pe.wait_ge(S["mul"], done(4 * g + u - 2))
                xs, j = u // 2, u % 2
                for n in range(2):
                    m = 2 * n + j
                    last = product(bank(2 * (u % 2) + n), w_parts[:, xs, m, 0, :], w_parts[:, xs, m, 1, :],
                                   x2T_hi[off % 2][:], x2T_lo[off % 2][:])
                last.then_inc(S["gu"], 1)

            def unit_down(i, off, u):
                g = 2 * i + off
                xs, j = u // 2, u % 2
                pe.wait_ge(S["hlo"], done(4 * g + u))
                if u == 0:
                    pe.wait_ge(S["yThi"], done(g - 1))
                product(bank(4), w_parts[:, xs, 4 + j, 0, :], w_parts[:, xs, 4 + j, 1, :], hT_hi[u % 2][:],
                        hT_lo[u % 2][:], start=u == 0, stop=u == 3).then_inc(S["yT"], 1)

            def shared_back(i, off):
                g = 2 * i + off
                pe.wait_ge(S["yThi"], done(g))
                pe.wait_ge(S["addb"], done(g - 1))
                for t in range(GT):
                    last = pe.transpose(bank(5, P, t * P), shT[:, t * P:(t + 1) * P], ident[:])
                last.then_inc(S["back"], 1)

            def shared_pe(i, off, route):
                unit_up(i, off, 2)
                unit_down(i, off, 0)
                if route:
                    t2(i, off + 1)
                unit_up(i, off, 3)
                unit_down(i, off, 1)
                if route:
                    logits_T(i, off + 1)
                    unit_up(i, off + 1, 0)
                    logits(i, off + 1)
                unit_down(i, off, 2)
                unit_down(i, off, 3)
                if route:
                    unit_up(i, off + 1, 1)
                    ranks(i, off + 1)
                shared_back(i, off)

            logits(0, 0)
            unit_up(0, 0, 0)
            unit_up(0, 0, 1)
            pe.wait_ge(S["x2"], done(NT - 1))
            ranks(0, 0)
            with pe.Fori(0, NG // 2 - 1) as i:
                shared_pe(i, 0, True)
                shared_pe(i, 1, True)
            shared_pe(NG // 2 - 1, 0, True)
            shared_pe(NG // 2 - 1, 1, False)

            def expert(word, off, m):
                return bass.ds(pe.snap((word >> (12 * (off % 2) + 3 * m)) & 7), 1)

            def x_transpose(i, off):
                p, par = 2 * i + off, off % 2
                for k in range(2):
                    pe.wait_ge(s_xg[2 * par + k], (i + off // 2 + 1) * 16)
                pe.wait_ge(S["xlo"], done(p - 1))
                for k in range(2):
                    last = pe.transpose(bank(4, P, k * P), xg[:, 2 * par + k, 0:C], ident[:])
                last.then_inc(S["tx"], 1)

            def up(i, off, k, word):
                p, par = 2 * i + off, off % 2
                if k == 0:
                    pe.wait_ge(S["xlo"], done(p))
                    pe.wait_ge(S["emul"], done(p - 2))
                e = expert(word, off, k)
                c = slice(k * P, (k + 1) * P)
                part = [w_parts[:, NSH:NX, 0:4, n, :][:, e, :, :].rearrange("p o m c -> p (o m) c") for n in range(2)]
                last = product(blocks(bank(2 * par + k)), gT_hi[par][:, c], gT_lo[par][:, c], part[0], part[1])
                if k:
                    last.then_inc(S["eh"], 1)

            def h_transpose(i, off):
                p, par = 2 * i + off, off % 2
                pe.wait_ge(S["emul"], done(p))
                pe.wait_ge(S["ehlo"], done(p - 1))
                for j in range(4):
                    last = pe.transpose(bank(5, P, j * P), hid[par][:, j * P:(j + 1) * P], ident[:])
                last.then_inc(S["eth"], 1)

            def down(i, off, k, word):
                p, par = 2 * i + off, off % 2
                if k == 0:
                    pe.wait_ge(S["ehlo"], done(p))
                pe.wait_ge(S["eyout"], done(2 * p + k - 2))
                e = expert(word, off + 1 + k, 2 + k)
                for j in range(2):
                    c = slice((2 * k + j) * P, (2 * k + j + 1) * P)
                    w2 = w_parts[:, NSH:NX, 4 + j, :, :]
                    pe.matmul(blocks(bank(6 + k, 2 * P)), hT_hi[par][:, c],
                              w2[:, e, :, :].rearrange("p o n c -> p (o n) c"), start=j == 0, stop=False)
                    last = pe.matmul(bank(6 + k, P), hT_lo[par][:, c],
                                     w2[:, e, 0, :].rearrange("p o c -> p (o c)"), start=False, stop=j == 1)
                last.then_inc(S["ey"], 1)

            def step_word(i):
                return pe.value_load(step_wi[0:1, bass.ds(i, 1)])

            def e_step(i, off, word, y1=True, h=True, x=True, y0=True, u=True):
                if y1:
                    down(i, off - 2, 1, word)
                if h:
                    h_transpose(i, off)
                if x:
                    x_transpose(i, off + 3)
                if u:
                    up(i, off + 2, 0, word)
                if y0:
                    down(i, off - 1, 0, word)
                if u:
                    up(i, off + 2, 1, word)

            pe.wait_ge(S["tab"], 1)
            pe.wait_ge(S["addb"], done(NG - 1))
            x_transpose(0, 0)
            x_transpose(0, 1)
            word = step_word(0)
            up(0, 0, 0, word)
            up(0, 0, 1, word)
            x_transpose(0, 2)
            up(0, 1, 0, word)
            up(0, 1, 1, word)
            word = step_word(1)
            e_step(0, 0, word, y1=False, y0=False)
            e_step(0, 1, word, y1=False)
            L = PAIRS // 2
            with pe.Fori(1, L - 2) as i:
                word = step_word(i + 1)
                e_step(i, 0, word)
                e_step(i, 1, word)
            word = step_word(L - 1)
            e_step(L - 2, 0, word)
            e_step(L - 2, 1, word, x=False)
            word = step_word(L)
            e_step(L - 1, 0, word, x=False, u=False)
            e_step(L - 1, 1, word, x=False, u=False)
            word = step_word(L + 1)
            e_step(L, 0, word, h=False, x=False, u=False)
            e_step(L, 1, word, h=False, x=False, y0=False, u=False)


INPUTS = ["L0_attn_x", "L0_attn_Wk", "L0_attn_Wq", "L0_attn_Wv", "L0_ffn_router_w", "L0_ffn_expert_bias",
          "L0_ffn_w1", "L0_ffn_w3", "L0_ffn_w2", "L0_ffn_sw1", "L0_ffn_sw3", "L0_ffn_sw2"]


def kernel(**inputs):
    import numpy as np
    import concourse.bacc as bacc
    from concourse.bass_utils import run_bass_kernel_spmd

    nc = bacc.Bacc("TRN2", target_bir_lowering=False, num_devices=1)
    arrays, args = {}, []
    for name in INPUTS:
        a = np.ascontiguousarray(inputs[name])
        arrays[name] = a
        args.append(nc.dram_tensor(name, a.shape, mybir.dt.from_np(a.dtype), kind="ExternalInput").ap())
    shape = arrays["L0_attn_x"].shape
    tokens, experts = shape[0] * shape[1], arrays["L0_ffn_w1"].shape[0]
    out = nc.dram_tensor("out", shape, F32, kind="ExternalOutput").ap()
    xbuf = nc.dram_tensor("xbuf", (experts * (tokens + P) + 8 * P, shape[2] + 2), F32).ap()
    ybuf = nc.dram_tensor("ybuf", (2 * tokens, shape[2]), F32).ap()
    build(nc, *args, out, xbuf, ybuf)
    r = run_bass_kernel_spmd(nc, [arrays], core_ids=[0])
    return r.results[0]["out"]
```
